# Optimizing a Trainium2 kernel written in Bass

```python
import numpy as np
import jax
import jax.numpy as jnp

def _softmax(x, axis=-1):
    return jax.nn.softmax(x, axis=axis)

def _gelu(x):
    return jax.nn.gelu(x, approximate=True)

def _silu(x):
    return jax.nn.silu(x)

def _sigmoid(x):
    return jax.nn.sigmoid(x)

def _layernorm(x, axis=-1, eps=1e-05):
    m = jnp.mean(x, axis=axis, keepdims=True)
    v = jnp.var(x, axis=axis, keepdims=True)
    return (x - m) / jnp.sqrt(v + eps)

def _scatter_add(tgt, idx, src, axis=0):
    return tgt.at[idx].add(src)

def _segment_sum(src, seg, n):
    return jax.ops.segment_sum(src, seg, n)
kernel_name = 'mk_audio_tower_d1_tok_audfeat768_r4_c3646a'

def setup_inputs(seed: int=0):
    np.random.seed(seed)
    _w = jnp.asarray

    def _rec_inputs():
        import jax
        import jax.numpy as jnp
        _rk = jax.random.key(seed)
        x = -0.000292821 + 1.00034 * jax.random.normal(jax.random.fold_in(_rk, 1), (128, 256, 8), jnp.float32)
        return x
    x = _rec_inputs()

    def _L0_tok_setup():
        import jax, jax.numpy as jnp
        import numpy as np
        PATCH_SIZE = 16
        STRIDE = 8
        N_CHANNELS = 8
        D_MODEL = 192
        key = jax.random.key(seed)
        kx, kw, kb = jax.random.split(key, 3)
        x = jax.random.normal(kx, (32, 4096, N_CHANNELS), dtype=jnp.float32)
        fan_in = PATCH_SIZE * N_CHANNELS
        bound = 1.0 / np.sqrt(fan_in)
        W = jax.random.uniform(kw, (D_MODEL, fan_in), dtype=jnp.float32, minval=-bound, maxval=bound)
        b = jax.random.uniform(kb, (D_MODEL,), dtype=jnp.float32, minval=-bound, maxval=bound)
        return {'x': x, 'W': W, 'b': b}
    _L0_tok_all = _L0_tok_setup()
    _L0_tok_in = {k: v for k, v in _L0_tok_all.items() if k in ('W', 'b')}
    del _L0_tok_all

    def _L0_attn_setup():
        import jax, jax.numpy as jnp
        import numpy as np
        import math
        B, T, C = (4, 512, 192)
        NH = 12
        D = C // NH
        key = jax.random.key(seed)
        k1, k2, k3 = jax.random.split(key, 3)
        s = 1.0 / math.sqrt(C)
        return {'x': jax.random.normal(k1, (B, T, C), dtype=jnp.float32), 'W_attn': jax.random.normal(k2, (C, 3 * C), dtype=jnp.float32) * s, 'b_attn': jnp.zeros((3 * C,), dtype=jnp.float32), 'W_proj': jax.random.normal(k3, (C, C), dtype=jnp.float32) * s, 'b_proj': jnp.zeros((C,), dtype=jnp.float32)}
    _L0_attn_all = _L0_attn_setup()
    _L0_attn_in = {k: v for k, v in _L0_attn_all.items() if k in ('W_attn', 'b_attn', 'W_proj', 'b_proj')}
    del _L0_attn_all

    def _L0_ffn_setup():
        import jax, jax.numpy as jnp
        import numpy as np
        H = 192
        R = 64
        E = 8
        B, S = (8, 512)
        key = jax.random.key(seed)
        ks = jax.random.split(key, 10)
        s_in = 1.0 / np.sqrt(H)
        s_r = 1.0 / np.sqrt(R)
        return {'x': jax.random.normal(ks[0], (B, S, H), dtype=jnp.float32), 'enc_w': jax.random.uniform(ks[1], (H, R), jnp.float32, -s_in, s_in), 'enc_b': jax.random.uniform(ks[2], (R,), jnp.float32, -s_in, s_in), 'sw_w': jax.random.uniform(ks[3], (R, E), jnp.float32, -s_r, s_r), 'sw_b': jax.random.uniform(ks[4], (E,), jnp.float32, -s_r, s_r), 'w1': jax.random.uniform(ks[5], (E, H, R), jnp.float32, -s_in, s_in), 'b1': jax.random.uniform(ks[6], (E, R), jnp.float32, -s_in, s_in), 'w2': jax.random.uniform(ks[7], (E, R, H), jnp.float32, -s_r, s_r), 'b2': jax.random.uniform(ks[8], (E, H), jnp.float32, -s_r, s_r)}
    _L0_ffn_all = _L0_ffn_setup()
    _L0_ffn_in = {k: v for k, v in _L0_ffn_all.items() if k in ('enc_w', 'enc_b', 'sw_w', 'sw_b', 'w1', 'b1', 'w2', 'b2')}
    del _L0_ffn_all
    return {'x': x, 'L0_tok_W': _L0_tok_in['W'], 'L0_tok_b': _L0_tok_in['b'], 'L0_attn_W_attn': _L0_attn_in['W_attn'], 'L0_attn_b_attn': _L0_attn_in['b_attn'], 'L0_attn_W_proj': _L0_attn_in['W_proj'], 'L0_attn_b_proj': _L0_attn_in['b_proj'], 'L0_ffn_enc_w': _L0_ffn_in['enc_w'], 'L0_ffn_enc_b': _L0_ffn_in['enc_b'], 'L0_ffn_sw_w': _L0_ffn_in['sw_w'], 'L0_ffn_sw_b': _L0_ffn_in['sw_b'], 'L0_ffn_w1': _L0_ffn_in['w1'], 'L0_ffn_b1': _L0_ffn_in['b1'], 'L0_ffn_w2': _L0_ffn_in['w2'], 'L0_ffn_b2': _L0_ffn_in['b2']}

def reference(x, L0_tok_W, L0_tok_b, L0_attn_W_attn, L0_attn_b_attn, L0_attn_W_proj, L0_attn_b_proj, L0_ffn_enc_w, L0_ffn_enc_b, L0_ffn_sw_w, L0_ffn_sw_b, L0_ffn_w1, L0_ffn_b1, L0_ffn_w2, L0_ffn_b2):
    import jax
    import jax.numpy as jnp

    def _L0_tok_ref(x, W, b):
        import jax, jax.numpy as jnp
        import numpy as np
        PATCH_SIZE = 16
        STRIDE = 8
        N_CHANNELS = 8
        D_MODEL = 192
        B, N, C = x.shape
        n_patches = 1 + (N - PATCH_SIZE) // STRIDE
        idx = jnp.arange(n_patches)[:, None] * STRIDE + jnp.arange(PATCH_SIZE)[None, :]
        patches = x[:, idx, :].reshape(B, n_patches, PATCH_SIZE * C)
        return jnp.einsum('bpk,dk->bpd', patches, W) + b

    def _L0_attn_ref(x, W_attn, b_attn, W_proj, b_proj):
        import jax, jax.numpy as jnp
        import numpy as np
        import math
        B, T, C = (4, 512, 192)
        NH = 12
        D = C // NH
        Bq, Tq, Cq = x.shape
        qkv = x @ W_attn + b_attn
        q, k, v = jnp.split(qkv, 3, axis=2)
        q = q.reshape(Bq, Tq, NH, D).transpose(0, 2, 1, 3)
        k = k.reshape(Bq, Tq, NH, D).transpose(0, 2, 1, 3)
        v = v.reshape(Bq, Tq, NH, D).transpose(0, 2, 1, 3)
        scores = jnp.einsum('bhtd,bhsd->bhts', q, k) / math.sqrt(D)
        causal = jnp.tril(jnp.ones((Tq, Tq), dtype=bool))
        scores = jnp.where(causal[None, None], scores, -jnp.inf)
        att = jax.nn.softmax(scores, axis=-1)
        y = jnp.einsum('bhts,bhsd->bhtd', att, v)
        y = y.transpose(0, 2, 1, 3).reshape(Bq, Tq, Cq)
        return y @ W_proj + b_proj

    def _L0_ffn_ref(x, enc_w, enc_b, sw_w, sw_b, w1, b1, w2, b2):
        import jax, jax.numpy as jnp
        import numpy as np
        H = 192
        R = 64
        E = 8
        B, S = (8, 512)
        b, s, d = x.shape
        xt = x.reshape(-1, d)
        x_enc = xt @ enc_w + enc_b
        route_prob = jax.nn.softmax(x_enc @ sw_w + sw_b, axis=-1)
        route_prob_max = jnp.max(route_prob, axis=-1)
        routes = jnp.argmax(route_prob, axis=-1)
        onehot = jax.nn.one_hot(routes, E, dtype=xt.dtype)
        h = jnp.einsum('td,edr->ter', xt, w1) + b1[None]
        h = jax.nn.gelu(h, approximate=False)
        h = h * onehot[..., None]
        out = jnp.einsum('ter,erd->td', h, w2) + onehot @ b2
        out = out * route_prob_max[:, None]
        return out.reshape(b, s, d)
    h = _L0_tok_ref(x, L0_tok_W, L0_tok_b)
    h = h + _L0_attn_ref(_layernorm(h, axis=-1), L0_attn_W_attn, L0_attn_b_attn, L0_attn_W_proj, L0_attn_b_proj)
    h = h + _L0_ffn_ref(_layernorm(h, axis=-1), L0_ffn_enc_w, L0_ffn_enc_b, L0_ffn_sw_w, L0_ffn_sw_b, L0_ffn_w1, L0_ffn_b1, L0_ffn_w2, L0_ffn_b2)
    return h

_drawn_inputs = setup_inputs


def setup_inputs(seed=0):
    import zlib

    import numpy as np

    out = dict(_drawn_inputs(seed))
    spreads = {'L0_attn_b_attn': (0.0, 0.1), 'L0_attn_b_proj': (0.0, 0.1)}
    factors = {'L0_ffn_enc_b': 5.428, 'L0_ffn_b1': 8.0, 'L0_ffn_b2': 3.143}
    for name, (base, spread) in spreads.items():
        noise = np.random.default_rng([zlib.crc32(name.encode()), seed]).standard_normal(out[name].shape)
        drawn = base * np.exp(spread * noise) if base else spread * noise
        out[name] = jnp.asarray(drawn.astype(out[name].dtype))
    for name, factor in factors.items():
        out[name] = (out[name] * factor).astype(out[name].dtype)
    return out
```

```python
from contextlib import ExitStack

import concourse.bass as bass
from concourse import mybir

F32 = mybir.dt.float32
F16 = mybir.dt.float16
BF16 = mybir.dt.bfloat16
ALU = mybir.AluOpType
ACT = mybir.ActivationFunctionType
AX_X = mybir.AxisListType.X
ds = bass.ds

P = 128
B, T_IN, C_IN = 128, 256, 8
STRIDE = 8
CH = STRIDE * C_IN
T = T_IN // STRIDE - 1
TP = 32
D = 192
H, HD = 12, 16
HA, HB = 8, 4
NB = P // TP
NG = B // NB
NPAIR = NG // 2
NBLK = NG // 4
E, R = 8, 64
ER = E * R
WS = 64.0
EPS = 1e-5
MASKED = -1e30
OFF = 32768.0 * WS
PW = 2 * P
BW = 4 * P


def audio_tower(nc, x, tok_w, tok_b, qkv_w, qk_b, v_b, proj_w, proj_b, enc_wt, enc_b, sw_w, sw_b,
                w1, b1, w2, b2, out):
    x_rows = x.rearrange("b (c t) f -> (b c) (t f)", t=STRIDE).rearrange("(g p) f -> p g f", p=P)

    with ExitStack() as ctx:
        def sb(name, shape, dt=F32):
            return ctx.enter_context(nc.sbuf_tensor(name, shape, dt))

        def sem(name):
            return ctx.enter_context(nc.semaphore(name))

        tok_w_f = sb("tok_w_f", [P, 2, D])
        qkv_w_f = sb("qkv_w_f", [P, 3, 3 * D])
        proj_w_f = sb("proj_w_f", [P, 3, D])
        w1_f = sb("w1_f", [P, 3, ER])
        w2_f = sb("w2_f", [P, 4, D])
        enc_wt_f = sb("enc_wt_f", [R, 3, P])
        enc_b_f = sb("enc_b_f", [R, 1])
        enc_b_wide = sb("enc_b_wide", [R, P])
        sw_w_f = sb("sw_w_f", [R, E])
        v_b_f = sb("v_b_f", [P, 2])
        v_b_wide = sb("v_b_wide", [P, 2, P])
        rows_f = sb("rows_f", [1, 2 * D + E])
        qk_b_f = sb("qk_b_f", [P, 3])
        qk_b_s = sb("qk_b_s", [P, 3])
        b1_f = sb("b1_f", [P, 4])
        b2_f = sb("b2_f", [40, D])
        tok_w_h = sb("tok_w_h", [P, 2, D], F16)
        tok_w_l = sb("tok_w_l", [P, 2, D], F16)
        qkv_h = sb("qkv_h", [P, 3, 3 * D], F16)
        qkv_l = sb("qkv_l", [P, 2, 3 * D], F16)
        proj_h = sb("proj_h", [P, 3, D], F16)
        proj_l = sb("proj_l", [P, 2, D], F16)
        w1_h = sb("w1_h", [P, 3, ER], F16)
        w1_l = sb("w1_l", [P, 2, ER], F16)
        w2_h = sb("w2_h", [P, 4, D], F16)
        w2_l = sb("w2_l", [P, 4, D], F16)
        router_f = sb("router_f", [P, 3, E])
        router_h = sb("router_h", [P, 3, E], F16)
        router_l = sb("router_l", [P, 2, E], F16)
        b2_h = sb("b2_h", [40, D], F16)
        b2_parts = sb("b2_parts", [40, D], F16)
        bias_rows = sb("bias_rows", [P, 2 * D + E])
        ident = sb("ident", [P, P], F16)
        causal = sb("causal", [P, H, TP], BF16)
        lower = sb("lower", [9, 4, P], BF16)
        ones_row = sb("ones_row", [1, P])
        pick = sb("pick", [P, E])
        x_f = sb("x_f", [P, NG, CH])
        x_s = sb("x_s", [P, NG, 2, CH], F16)
        xT = sb("xT", [P, PW + 1], F16)
        h_all = sb("h_all", [P, NPAIR, 2, D])
        stats = sb("stats", [P, 2, 2, 6])
        mv = sb("mv", [P, 2, 2, 2])
        var_eps = sb("var_eps", [P, 2, 2])
        half = sb("half", [P, 2])
        rstd = sb("rstd", [P, 2, 2])
        xn_f = sb("xn_f", [P, 2, D])
        xn_s = sb("xn_s", [P, 2, 2, D], F16)
        xnT = sb("xnT", [P, 3, PW], F16)
        qk_s = [sb(f"qk_s{u}", [P, 3, 2, PW], F16) for u in range(2)]
        v_s = [sb(f"v_s{u}", [P, 2, 2, H, HD + 1], F16) for u in range(2)]
        k_a = [sb(f"k_a{u}", [P, 2, HA, PW], F16) for u in range(2)]
        k_b = [sb(f"k_b{u}", [HB * HD, 2, HB, PW], F16) for u in range(2)]
        top = sb("top", [P, 2, H])
        scores = sb("scores", [P, 2, H, TP])
        prob = sb("prob", [P, 2, H, TP])
        probT = sb("probT", [P, 2, TP, H])
        probT_s = sb("probT_s", [P, 2, 2, TP, H], F16)
        p_mem = [sb(f"p_mem{u}", [P, 4 * P * H], F16) for u in range(2)]
        p_bd = [m[:].rearrange("p (g k c h) -> p g k c h", g=2, k=2, h=H) for m in p_mem]
        rden = sb("rden", [P, 2, H])
        y_f = sb("y_f", [P, 2, H, HD])
        y_s = sb("y_s", [P, 2, 2, D], F16)
        yT = sb("yT", [P, 3, PW], F16)
        h = sb("h", [P, 2, D])
        h2 = sb("h2", [P, 2, D])
        spacer = sb("spacer", [P, 1])
        x2_f = sb("x2_f", [P, 2, D])
        x2_s = sb("x2_s", [P, 2, 2, D], F16)
        x2T = sb("x2T", [P, 3, NG * P], F16)
        logit = sb("logit", [P, NG, E])
        l_top = sb("l_top", [P, NG])
        l_exp = sb("l_exp", [P, NG, E])
        l_sum = sb("l_sum", [P, NG])
        p_top = sb("p_top", [P, NG])
        cand = sb("cand", [P, NG, E])
        c_top = sb("c_top", [P, NG])
        onehot = x_s[:].rearrange("p g k c -> p g (k c)")
        ohT = [sb(f"ohT{u}", [64, BW], F16) for u in range(2)]
        g_f = [x_f[:].rearrange("p g c -> p (g c)")[:, u * BW:(u + 1) * BW] for u in range(2)]
        g_h = [m[:, 0:4 * BW].rearrange("p (j c) -> p j c", j=4) for m in p_mem]
        g_l = [m[:, 4 * BW:8 * BW].rearrange("p (j c) -> p j c", j=4) for m in p_mem]
        o_f = [m[:, 8 * BW:8 * BW + 8 * D].bitcast(F32).rearrange("p (g d) -> p g d", g=4) for m in p_mem]

        bank = [ctx.enter_context(nc.psum_tensor(f"bank{i}", [P, 512], F32)) for i in range(8)]
        t0 = bank[0][:].bitcast(F16).rearrange("p (k c) -> p k c", k=4)
        t1 = bank[1][:].bitcast(F16).rearrange("p (k c) -> p k c", k=4)
        hv = bank[2]
        yp = bank[3]
        qk01, qk2 = bank[4], bank[5]
        sc = [bank[6], bank[7]]
        pre = [bank[2], bank[3], bank[4], bank[5]]
        ffn = [bank[6], bank[7]]

        w_load = {n: sem(f"{n}_load") for n in ("tok", "qkv", "rest")}
        x_load = [sem(f"x_load{i}") for i in range(4)]
        consts = sem("consts")
        zeroed = sem("zeroed")
        zeroed_d = sem("zeroed_d")
        small = sem("small")
        wide = sem("wide")
        folded = sem("folded")
        split_a = sem("split_a")
        split_d = sem("split_d")
        x_hi = sem("x_hi")
        x_lo = sem("x_lo")
        xT_ps, xT_sb = sem("xT_ps"), sem("xT_sb")
        tok_ps, h_sb = sem("tok_ps"), sem("h_sb")
        bn1, ag1, rs1, xn_sb, xn_hi, xn_lo = (sem(n) for n in ("bn1", "ag1", "rs1", "xn_sb", "xn_hi", "xn_lo"))
        ve1, ve2 = sem("ve1"), sem("ve2")
        xnT_ps, xnT_sb = sem("xnT_ps"), sem("xnT_sb")
        qk_ps, qk_hi, qk_lo = sem("qk_ps"), sem("qk_hi"), sem("qk_lo")
        v_ps, v_hi, v_lo = sem("v_ps"), sem("v_hi"), sem("v_lo")
        k_bd = sem("k_bd")
        sc_ps, sc_top, sc_sb = sem("sc_ps"), sem("sc_top"), sem("sc_sb")
        pr_sb, pT_sb, pT_hi, pT_lo, pT_bd = (sem(n) for n in ("pr_sb", "pT_sb", "pT_hi", "pT_lo", "pT_bd"))
        pv_ps, rden_sb, y_sb, y_hi, y_lo = (sem(n) for n in ("pv_ps", "rden_sb", "y_sb", "y_hi", "y_lo"))
        yT_ps, yT_sb = sem("yT_ps"), sem("yT_sb")
        hb_sb, proj_ps, h2_sb, h2_kept = sem("hb_sb"), sem("proj_ps"), sem("h2_sb"), sem("h2_kept")
        bn2, ag2, rs2, x2_sb, x2_hi, x2_lo = (sem(n) for n in ("bn2", "ag2", "rs2", "x2_sb", "x2_hi", "x2_lo"))
        x2T_ps, x2T_sb = sem("x2T_ps"), sem("x2T_sb")
        logit_ps, router_d, router_a = sem("logit_ps"), sem("router_d"), sem("router_a")
        ohT_ps, ohT_sb = sem("ohT_ps"), sem("ohT_sb")
        pre_ps, g_sb, gh_sb, gl_sb = sem("pre_ps"), sem("g_sb"), sem("gh_sb"), sem("gl_sb")
        ffn_ps, o_sb, stored = sem("ffn_ps"), sem("o_sb"), sem("stored")

        X_CUTS = [0, 2, 8, 16, NG]

        def at_least(eng, s, n):
            if not isinstance(n, int) or n > 0:
                eng.wait_ge(s, n)

        def pipeline(eng, step, n, ahead):
            first = ahead + 2 + ahead % 2
            last = n - n % 2
            for t in range(first):
                step(t, t % 2)
            with eng.Fori(first // 2, last // 2) as i:
                for u in range(2):
                    step(2 * i + u, u)
            for t in range(last, n + ahead):
                step(t, t % 2)

        def runs(t, lag, n):
            return not isinstance(t, int) or 0 <= t - lag < n

        block = ctx.enter_context(nc.Block())

        @block.sync
        def _(sp):
            sp.dma_start(x_f[:, 0:2, :], x_rows[:, 0:2, :]).then_inc(x_load[0], 16)
            sp.dma_start(tok_w_f[:], tok_w).then_inc(w_load["tok"], 16)
            sp.dma_start(qkv_w_f[:], qkv_w).then_inc(w_load["qkv"], 16)
            for i in range(1, 4):
                a, b = X_CUTS[i], X_CUTS[i + 1]
                sp.dma_start(x_f[:, a:b, :], x_rows[:, a:b, :]).then_inc(x_load[i], 16)
            sp.dma_start(w1_f[:], w1).then_inc(w_load["rest"], 16)
            sp.dma_start(w2_f[:], w2).then_inc(w_load["rest"], 16)

            def step(t, u):
                if runs(t, 1, NPAIR):
                    sp.wait_ge(pT_hi, t)
                    sp.wait_ge(pT_lo, t)
                    for b in range(NB):
                        r = slice(b * TP, (b + 1) * TP)
                        sp.dma_start(p_bd[1 - u][r, :, :, r, :], probT_s[r]).then_inc(pT_bd, 16)
                if runs(t, 0, NPAIR):
                    sp.wait_ge(qk_hi, 2 * t + 2)
                    sp.wait_ge(qk_lo, 2 * t + 2)
                    for h in range(HA):
                        r = slice(h * HD, (h + 1) * HD)
                        sp.dma_start(k_a[u][r, :, h, :], qk_s[u][r, 1, :, :]).then_inc(k_bd, 16)
                    for h in range(HB):
                        r = slice(h * HD, (h + 1) * HD)
                        s = slice(R + h * HD, R + (h + 1) * HD)
                        sp.dma_start(k_b[u][r, :, h, :], qk_s[u][s, 2, :, :]).then_inc(k_bd, 16)
                if runs(t, 2, NPAIR):
                    sp.wait_ge(h2_sb, t - 1)
                    sp.dma_start(h_all[:, t - 2], h2[:]).then_inc(h2_kept, 16)

            sp.wait_ge(zeroed, 2)
            sp.wait_ge(zeroed_d, 1)
            pipeline(sp, step, NPAIR, 2)

            for s in range(NBLK):
                sp.wait_ge(o_sb, s + 1)
                at_least(sp, stored, 16 * NB * s)
                for b in range(NB):
                    dst = out.rearrange("(s g b) t d -> s b t g d", g=4, b=NB)[s, b]
                    sp.dma_start(dst, o_f[s % 2][b * TP:b * TP + T, :, :]).then_inc(stored, 16)
            sp.wait_ge(stored, 16 * NB * NBLK)

        @block.gpsimd
        def _(pool):
            made = [0]

            def make(ins):
                ins.then_inc(consts, 1)
                made[0] += 1
                pool.wait_ge(consts, made[0])

            make(pool.memset(half[:], -0.5))
            make(pool.memset(ident[:], 0.0))
            make(pool.affine_select(out=ident[:], in_=ident[:], compare_op=ALU.not_equal, fill=1.0, base=0,
                                    pattern=[[-1, P]], channel_multiplier=1))
            make(pool.memset(causal[:], 0.0))
            for b in range(NB):
                r = slice(b * TP, (b + 1) * TP)
                make(pool.affine_select(out=causal[r], in_=causal[r], compare_op=ALU.is_ge, fill=MASKED, base=0,
                                        pattern=[[0, H], [-1, TP]], channel_multiplier=1))
            make(pool.memset(lower[:], -OFF))
            make(pool.memset(lower[0:E], 0.0))
            lower_e = lower[0:E].rearrange("e j (k c) -> e j k c", k=2)
            make(pool.affine_select(out=lower_e, in_=lower_e, compare_op=ALU.not_equal, fill=OFF, base=0,
                                    pattern=[[-2, 4], [-1, 2], [0, R]], channel_multiplier=1))
            for u in range(2):
                pool.memset(p_mem[u][:].bitcast(F32), 0.0).then_inc(zeroed, 1)
            for dst, src in ((rows_f[:, 0:D], tok_b), (rows_f[:, D:2 * D], proj_b),
                             (rows_f[:, 2 * D:2 * D + E], sw_b), (qk_b_f[:], qk_b), (v_b_f[:], v_b),
                             (enc_wt_f[:], enc_wt), (enc_b_f[:], enc_b), (sw_w_f[:], sw_w),
                             (b1_f[:], b1), (b2_f[0:E], b2), (b2_f[32:32 + E], b2), (proj_w_f[:], proj_w)):
                pool.dma_start(dst, src).then_inc(small, 16)

            def step(t, u):
                if runs(t, 2, NPAIR):
                    pool.wait_ge(y_hi, t - 1)
                    pool.tensor_tensor(y_s[:, :, 1, :], y_f[:].rearrange("p g h d -> p g (h d)"), y_s[:, :, 0, :],
                                       ALU.subtract).then_inc(y_lo, 1)
                if runs(t, 0, NPAIR):
                    if isinstance(t, int) and t == 0:
                        pool.wait_ge(folded, 3)
                    pool.wait_ge(ve1, t + 1)
                    pool.tensor_tensor(rstd[:, 0, :], var_eps[:, 0, :], half[:], ALU.pow).then_inc(rs1, 1)
                    pool.tensor_tensor(h_all[:, t], h[:], bias_rows[:, D:2 * D].unsqueeze(1).to_broadcast([P, 2, D]),
                                       ALU.add).then_inc(hb_sb, 1)
                    pool.wait_ge(xn_hi, t + 1)
                    pool.tensor_tensor(xn_s[:, :, 1, :], xn_f[:], xn_s[:, :, 0, :], ALU.subtract).then_inc(xn_lo, 1)
                if runs(t, 2, NPAIR):
                    pool.wait_ge(ve2, t - 1)
                    pool.tensor_tensor(rstd[:, 1, :], var_eps[:, 1, :], half[:], ALU.pow).then_inc(rs2, 1)
                if runs(t, 1, NPAIR):
                    pool.wait_ge(pT_hi, t)
                    pool.tensor_tensor(probT_s[:, :, 1], probT[:], probT_s[:, :, 0], ALU.subtract).then_inc(pT_lo, 1)
                if runs(t, 2, NPAIR):
                    pool.wait_ge(x2_hi, t - 1)
                    pool.tensor_tensor(x2_s[:, :, 1, :], x2_f[:], x2_s[:, :, 0, :], ALU.subtract).then_inc(x2_lo, 1)

            pipeline(pool, step, NPAIR, 2)

        @block.scalar
        def _(act):
            def hi(dst, src):
                return act.activation(dst, src, ACT.Copy, scale=WS)

            act.wait_ge(x_load[0], 16)
            act.copy(x_s[:, 0:2, 0, :], x_f[:, 0:2, :]).then_inc(x_hi, 1)
            act.wait_ge(w_load["tok"], 16)
            hi(tok_w_h[:], tok_w_f[:]).then_inc(split_a, 1)
            act.wait_ge(w_load["qkv"], 16)
            hi(qkv_h[:], qkv_w_f[:]).then_inc(split_a, 1)
            for i in range(1, 4):
                a, b = X_CUTS[i], X_CUTS[i + 1]
                act.wait_ge(x_load[i], 16)
                act.copy(x_s[:, a:b, 0, :], x_f[:, a:b, :]).then_inc(x_hi, 1)
            act.wait_ge(small, 16 * 12)
            hi(proj_h[:], proj_w_f[:]).then_inc(split_a, 1)
            hi(qk_b_s[:], qk_b_f[:]).then_inc(split_a, 1)
            hi(b2_h[0:E], b2_f[0:E])
            hi(b2_h[32:32 + E], b2_f[32:32 + E]).then_inc(split_a, 1)
            act.wait_ge(w_load["rest"], 32)
            hi(w1_h[:], w1_f[:]).then_inc(split_a, 1)
            hi(w2_h[:], w2_f[:]).then_inc(split_a, 1)
            act.wait_ge(folded, 2)
            hi(router_h[:], router_f[:]).then_inc(split_a, 1)

            def step(t, u):
                if runs(t, 0, NPAIR):
                    act.wait_ge(xT_ps, t + 1)
                    at_least(act, tok_ps, t)
                    act.copy(xT[:, 0:PW].rearrange("p (g c) -> p g c", g=2), t0[:, 3:4, :].rearrange("p o (g c) -> p (o g) c", g=2)).then_inc(xT_sb, 1)
                if runs(t, 2, NPAIR):
                    act.wait_ge(y_sb, t - 1)
                    at_least(act, yT_ps, t - 2)
                    act.copy(y_s[:, :, 0, :], y_f[:].rearrange("p g h d -> p g (h d)")).then_inc(y_hi, 1)
                if runs(t, 0, NPAIR):
                    act.wait_ge(xn_sb, t + 1)
                    at_least(act, xnT_ps, t)
                    act.copy(xn_s[:, :, 0, :], xn_f[:]).then_inc(xn_hi, 1)
                if runs(t, 2, NPAIR):
                    act.wait_ge(yT_ps, t - 1)
                    at_least(act, proj_ps, t - 2)
                    act.copy(yT[:], t1[:, 0:3, :]).then_inc(yT_sb, 1)
                if runs(t, 0, NPAIR):
                    act.wait_ge(xnT_ps, t + 1)
                    at_least(act, v_ps, t)
                    act.copy(xnT[:], t0[:, 0:3, :]).then_inc(xnT_sb, 1)
                if runs(t, 1, NPAIR):
                    act.wait_ge(sc_sb, t)
                    at_least(act, pT_sb, t - 1)
                    act.activation(prob[:], scores[:], ACT.Exp, scale=0.25 / (WS * WS)).then_inc(pr_sb, 1)
                if runs(t, 0, NPAIR):
                    act.wait_ge(qk_ps, 2 * t + 1)
                    for j in range(2):
                        mm = act.activation(qk_s[u][:, j, 0, :], qk01[:, j * PW:(j + 1) * PW], ACT.Identity,
                                            bias=qk_b_s[:, j:j + 1])
                    mm.then_inc(qk_hi, 1)
                    act.wait_ge(qk_ps, 2 * t + 2)
                    act.activation(qk_s[u][:, 2, 0, :], qk2[:, 0:PW], ACT.Identity, bias=qk_b_s[:, 2:3]).then_inc(qk_hi, 1)
                if runs(t, 1, NPAIR):
                    act.wait_ge(pT_sb, t)
                    at_least(act, pT_bd, 16 * NB * (t - 1) if not isinstance(t, int) or t > 1 else 0)
                    act.copy(probT_s[:, :, 0], probT[:]).then_inc(pT_hi, 1)
                if runs(t, 0, NPAIR):
                    act.wait_ge(v_ps, t + 1)
                    act.copy(v_s[u][:, :, 0, :, 0:HD], hv[:, 0:2 * D].rearrange("p (g h d) -> p g h d", g=2, h=H)).then_inc(v_hi, 1)
                if runs(t, 2, NPAIR):
                    act.wait_ge(x2_sb, t - 1)
                    at_least(act, x2T_ps, t - 2)
                    act.copy(x2_s[:, :, 0, :], x2_f[:]).then_inc(x2_hi, 1)
                    act.wait_ge(x2T_ps, t - 1)
                    act.copy(x2T[:, :, ds((t - 2) * PW, PW)], t1[:, 0:3, :]).then_inc(x2T_sb, 1)

            pipeline(act, step, NPAIR, 2)

            act.wait_ge(router_d, 3)
            act.activation(l_exp[:], l_exp[:], ACT.Exp).then_inc(router_a, 1)

            def ffn_step(s, u):
                if runs(s, 0, NBLK):
                    act.wait_ge(ohT_ps, s + 1)
                    act.copy(ohT[u][:], t0[0:64, 0:2, :].rearrange("p k c -> p (k c)")).then_inc(ohT_sb, 1)
                    for j in range(4):
                        act.wait_ge(pre_ps, 4 * s + j + 1)
                        at_least(act, gl_sb, 4 * s + j - 1 if not isinstance(s, int) or 4 * s + j > 1 else 0)
                        act.activation(g_f[j % 2], pre[j][:], ACT.Gelu, bias=b1_f[:, j:j + 1], scale=1.0 / WS).then_inc(g_sb, 1)
                        act.activation(g_h[u][:, j, :], pre[j][:], ACT.Gelu, bias=b1_f[:, j:j + 1], scale=1.0 / WS).then_inc(gh_sb, 1)

            pipeline(act, ffn_step, NBLK, 1)

        @block.vector
        def _(dve):
            def lo(dst, src, high):
                return dve.scalar_tensor_tensor(out=dst, in0=src, scalar=WS, in1=high, op0=ALU.mult, op1=ALU.subtract)

            for u in range(2):
                dve.memset(k_a[u][:].bitcast(F32), 0.0)
                dve.memset(k_b[u][:].bitcast(F32), 0.0)
                dve.memset(v_s[u][:, :, 0, :, HD:HD + 1], WS)
                dve.memset(v_s[u][:, :, 1, :, HD:HD + 1], 0.0)
            dve.memset(b2_parts[:], 0.0)
            dve.memset(xT[:, PW:PW + 1], 0.0)
            dve.memset(ones_row[:], 1.0).then_inc(zeroed_d, 1)
            dve.wait_ge(zeroed_d, 1)
            dve.wait_ge(x_hi, 1)
            dve.tensor_tensor(x_s[:, 0:2, 1, :], x_f[:, 0:2, :], x_s[:, 0:2, 0, :], ALU.subtract).then_inc(x_lo, 1)
            dve.wait_ge(split_a, 1)
            lo(tok_w_l[:], tok_w_f[:], tok_w_h[:]).then_inc(split_d, 1)
            dve.wait_ge(small, 16 * 12)
            dve.tensor_scalar(enc_b_wide[:], enc_b_f[:].to_broadcast([R, P]), 1.0, None, ALU.mult).then_inc(wide, 1)
            dve.tensor_copy(v_b_wide[:], v_b_f[:].unsqueeze(2).to_broadcast([P, 2, P])).then_inc(wide, 1)
            dve.wait_ge(split_a, 2)
            lo(qkv_l[:], qkv_w_f[:, 0:2, :], qkv_h[:, 0:2, :]).then_inc(split_d, 1)
            for i in range(1, 4):
                a, b = X_CUTS[i], X_CUTS[i + 1]
                dve.wait_ge(x_hi, i + 1)
                dve.tensor_tensor(x_s[:, a:b, 1, :], x_f[:, a:b, :], x_s[:, a:b, 0, :], ALU.subtract).then_inc(x_lo, 1)
            dve.wait_ge(split_a, 5)
            lo(proj_l[:], proj_w_f[:, 0:2, :], proj_h[:, 0:2, :]).then_inc(split_d, 1)
            dve.tensor_copy(b2_parts[0:E], b2_h[0:E]).then_inc(split_d, 1)
            lo(b2_parts[32:32 + E], b2_f[32:32 + E], b2_h[32:32 + E]).then_inc(split_d, 1)
            dve.wait_ge(folded, 1)
            dve.tensor_copy(router_f[:], pre[0][:, 0:3 * E].rearrange("p (k e) -> p k e", k=3)).then_inc(folded, 1)
            dve.tensor_copy(bias_rows[:], pre[1][:, 0:2 * D + E]).then_inc(folded, 1)
            dve.wait_ge(split_a, 8)
            lo(w1_l[:], w1_f[:, 0:2, :], w1_h[:, 0:2, :]).then_inc(split_d, 1)
            lo(w2_l[:], w2_f[:], w2_h[:]).then_inc(split_d, 1)
            lo(router_l[:], router_f[:, 0:2, :], router_h[:, 0:2, :]).then_inc(split_d, 1)
            dve.wait_ge(folded, 3)

            def norm(p, k, h_row, dst, bn, ag, ve, rs, done):
                for g in range(2):
                    dve.bn_stats(stats[:, k, g, :], h_row[:, g, :]).then_inc(bn, 1)
                dve.wait_ge(bn, 2 * p + 2)
                dve.memset(spacer[:], 0.0)
                for g in range(2):
                    dve.bn_aggr(mv[:, k, g, :], stats[:, k, g, :]).then_inc(ag, 1)
                dve.wait_ge(ag, 2 * p + 2)
                dve.tensor_scalar(var_eps[:, k, :], mv[:, k, :, 1], EPS, None, ALU.add).then_inc(ve, 1)
                dve.wait_ge(rs, p + 1)
                for g in range(2):
                    mm = dve.tensor_scalar(dst[:, g, :], h_row[:, g, :], mv[:, k, g, 0:1], rstd[:, k, g:g + 1],
                                           ALU.subtract, ALU.mult)
                mm.then_inc(done, 1)

            def step(t, u):
                if runs(t, 2, NPAIR):
                    p = t - 2
                    dve.wait_ge(pv_ps, p + 1)
                    yv = yp[:, 0:2 * H * (HD + 1)].rearrange("p (g h d) -> p g h d", g=2, h=H)
                    dve.reciprocal(rden[:], yv[:, :, :, HD]).then_inc(rden_sb, 1)
                    dve.wait_ge(rden_sb, p + 1)
                    at_least(dve, y_lo, p)
                    at_least(dve, y_hi, p)
                    dve.tensor_tensor(y_f[:], yv[:, :, :, 0:HD], rden[:].unsqueeze(3).to_broadcast([P, 2, H, HD]),
                                      ALU.mult).then_inc(y_sb, 1)
                if runs(t, 0, NPAIR):
                    dve.wait_ge(tok_ps, t + 1)
                    at_least(dve, hb_sb, t)
                    dve.scalar_tensor_tensor(out=h[:], in0=hv[:, 0:2 * D].rearrange("p (g d) -> p g d", g=2),
                                             scalar=1.0 / WS, in1=bias_rows[:, 0:D].unsqueeze(1).to_broadcast([P, 2, D]),
                                             op0=ALU.mult, op1=ALU.add).then_inc(h_sb, 1)
                    dve.wait_ge(h_sb, t + 1)
                    at_least(dve, xn_hi, t)
                    at_least(dve, xn_lo, t)
                    norm(t, 0, h, xn_f, bn1, ag1, ve1, rs1, xn_sb)
                if runs(t, 1, NPAIR):
                    p = t - 1
                    at_least(dve, pr_sb, p)
                    for g in range(2):
                        s = sc[g][:, 0:H * TP].rearrange("p (h s) -> p h s", h=H)
                        dve.wait_ge(sc_ps, 2 * p + g + 1)
                        dve.tensor_reduce(top[:, g, :], s, AX_X, ALU.max).then_inc(sc_top, 1)
                    for g in range(2):
                        s = sc[g][:, 0:H * TP].rearrange("p (h s) -> p h s", h=H)
                        dve.wait_ge(sc_top, 2 * p + g + 1)
                        mm = dve.tensor_tensor(scores[:, g], s, top[:, g, :].unsqueeze(2).to_broadcast([P, H, TP]),
                                               ALU.subtract)
                    mm.then_inc(sc_sb, 1)
                if runs(t, 2, NPAIR):
                    p = t - 2
                    dve.wait_ge(proj_ps, p + 1)
                    dve.wait_ge(hb_sb, p + 1)
                    at_least(dve, h2_kept, 16 * p)
                    dve.scalar_tensor_tensor(out=h2[:], in0=yp[:, 0:2 * D].rearrange("p (g d) -> p g d", g=2),
                                             scalar=1.0 / WS, in1=h_all[:, p], op0=ALU.mult, op1=ALU.add).then_inc(h2_sb, 1)
                    dve.wait_ge(h2_sb, p + 1)
                    at_least(dve, x2_hi, p)
                    at_least(dve, x2_lo, p)
                    norm(p, 1, h2, x2_f, bn2, ag2, ve2, rs2, x2_sb)
                if runs(t, 1, NPAIR):
                    p = t - 1
                    dve.wait_ge(pr_sb, p + 1)
                    at_least(dve, pT_hi, p)
                    at_least(dve, pT_lo, p)
                    dve.transpose(probT[:].rearrange("p g t h -> p g h t"), prob[:]).then_inc(pT_sb, 1)
                if runs(t, 0, NPAIR):
                    for j in range(3):
                        if j != 1:
                            dve.wait_ge(qk_hi, 2 * t + 1 + j // 2)
                        src = qk01[:, j * PW:(j + 1) * PW] if j < 2 else qk2[:, 0:PW]
                        mm = dve.scalar_tensor_tensor(out=qk_s[u][:, j, 1, :], in0=src, scalar=qk_b_s[:, j:j + 1],
                                                      in1=qk_s[u][:, j, 0, :], op0=ALU.add, op1=ALU.subtract)
                        if j > 0:
                            mm.then_inc(qk_lo, 1)
                    dve.wait_ge(v_hi, t + 1)
                    dve.tensor_tensor(v_s[u][:, :, 1, :, 0:HD], hv[:, 0:2 * D].rearrange("p (g h d) -> p g h d", g=2, h=H),
                                      v_s[u][:, :, 0, :, 0:HD], ALU.subtract).then_inc(v_lo, 1)

            pipeline(dve, step, NPAIR, 2)

            dve.wait_ge(logit_ps, 1)
            dve.wait_ge(h2_kept, 16 * NPAIR)
            dve.scalar_tensor_tensor(out=logit[:], in0=hv[:, 0:NG * E].rearrange("p (g e) -> p g e", e=E), scalar=1.0 / WS,
                                     in1=bias_rows[:, 2 * D:2 * D + E].unsqueeze(1).to_broadcast([P, NG, E]),
                                     op0=ALU.mult, op1=ALU.add).then_inc(router_d, 1)
            dve.wait_ge(router_d, 1)
            dve.tensor_reduce(l_top[:], logit[:], AX_X, ALU.max).then_inc(router_d, 1)
            dve.wait_ge(router_d, 2)
            l_top_w = l_top[:].unsqueeze(2).to_broadcast([P, NG, E])
            dve.tensor_tensor(l_exp[:], logit[:], l_top_w, ALU.subtract).then_inc(router_d, 1)
            dve.tensor_tensor(cand[:], logit[:], l_top_w, ALU.is_equal).then_inc(router_d, 1)
            dve.memset(onehot, 0.0).then_inc(router_d, 1)
            for e in range(E):
                dve.memset(pick[:, e:e + 1], float(E - e)).then_inc(router_d, 1)
            dve.wait_ge(router_d, 5 + E)
            dve.tensor_tensor(cand[:], cand[:], pick[:].unsqueeze(1).to_broadcast([P, NG, E]), ALU.mult).then_inc(router_d, 1)
            dve.wait_ge(router_d, 6 + E)
            dve.tensor_reduce(c_top[:], cand[:], AX_X, ALU.max).then_inc(router_d, 1)
            dve.wait_ge(router_d, 7 + E)
            for c in (0, 32):
                dve.tensor_tensor(onehot[:, :, c:c + E], cand[:], c_top[:].unsqueeze(2).to_broadcast([P, NG, E]),
                                  ALU.is_equal).then_inc(router_d, 1)
            dve.memset(onehot[:, :, E:E + 1], 1.0).then_inc(router_d, 1)
            dve.wait_ge(router_a, 1)
            dve.tensor_reduce(l_sum[:], l_exp[:], AX_X, ALU.add).then_inc(router_d, 1)
            dve.wait_ge(router_d, 11 + E)
            dve.reciprocal(l_top[:], l_sum[:]).then_inc(router_d, 1)
            dve.wait_ge(router_d, 12 + E)
            dve.tensor_scalar(p_top[:], l_top[:], 1.0 / WS, None, ALU.mult).then_inc(router_d, 1)
            dve.wait_ge(router_d, 13 + E)

            def ffn_step(s, u):
                if runs(s, 0, NBLK):
                    for j in range(4):
                        dve.wait_ge(gh_sb, 4 * s + j + 1)
                        dve.tensor_tensor(g_l[u][:, j, :], g_f[j % 2], g_h[u][:, j, :], ALU.subtract).then_inc(gl_sb, 1)
                if runs(s, 1, NBLK):
                    q = s - 1
                    at_least(dve, stored, 16 * NB * (q - 1) if not isinstance(q, int) or q > 1 else 0)
                    for g in range(4):
                        if g % 2 == 0:
                            dve.wait_ge(ffn_ps, 2 * q + g // 2 + 1)
                        mm = dve.scalar_tensor_tensor(out=o_f[1 - u][:, g, :], in0=ffn[g // 2][:, (g % 2) * D:(g % 2 + 1) * D],
                                                      scalar=p_top[:, ds(4 * q + g, 1)], in1=h_all[:, ds(2 * q + g // 2, 1), g % 2, :].rearrange("p o d -> p (o d)"),
                                                      op0=ALU.mult, op1=ALU.add)
                    mm.then_inc(o_sb, 1)

            pipeline(dve, ffn_step, NBLK, 1)

        @block.tensor
        def _(pe):
            pe.wait_ge(wide, 2)
            pe.wait_ge(zeroed, 2)
            pe.wait_ge(zeroed_d, 1)
            for k in range(3):
                pe.matmul(pre[0][:, k * E:(k + 1) * E], enc_wt_f[:, k, :], sw_w_f[:], start=(k == 0), stop=True,
                          skip_group_check=True)
            pe.matmul(pre[1][:, 0:D], ones_row[:], rows_f[:, 0:D], start=True, stop=True)
            pe.matmul(pre[1][:, D:2 * D], v_b_wide[:, 0, :], proj_w_f[:, 0, :], start=False, stop=False, skip_group_check=True)
            pe.matmul(pre[1][:, D:2 * D], v_b_wide[0:R, 1, :], proj_w_f[0:R, 1, :], start=False, stop=False, skip_group_check=True)
            pe.matmul(pre[1][:, D:2 * D], ones_row[:], rows_f[:, D:2 * D], start=False, stop=True, skip_group_check=True)
            pe.matmul(pre[1][:, 2 * D:2 * D + E], enc_b_wide[:], sw_w_f[:], start=False, stop=False, skip_group_check=True)
            pe.matmul(pre[1][:, 2 * D:2 * D + E], ones_row[:], rows_f[:, 2 * D:2 * D + E], start=False, stop=True,
                      skip_group_check=True).then_inc(folded, 1)
            pe.wait_ge(folded, 3)
            pe.wait_ge(consts, 11)
            pe.wait_ge(split_d, 8)

            def parts(w_h, w_l):
                return [(0, w_h[:, 0]), (1, w_h[:, 1]), (2, w_h[:, 2]), (0, w_l[:, 0]), (1, w_l[:, 1])]

            def rows_by_weights(dst, actT, c0, w_h, w_l, cols):
                five = parts(w_h, w_l)
                for n, (k, w) in enumerate(five):
                    mm = pe.matmul(dst, actT[:, k, c0:c0 + P], w[:, cols], start=(n == 0), stop=(n == 4))
                return mm

            def turn(bank_t, src, c0):
                for k in range(3):
                    mm = pe.transpose(bank_t[:, k, c0:c0 + P], src[:, k * P:(k + 1) * P], ident[:])
                return mm

            def step(t, u):
                if runs(t, 0, NPAIR):
                    at_least(pe, xnT_sb, t)
                    if isinstance(t, int):
                        pe.wait_ge(x_lo, 1 if t < 1 else 4)
                    for g in range(2):
                        mm = pe.transpose(t0[:, 3, g * P:(g + 1) * P],
                                          x_s[:, ds(2 * t + g, 1)].rearrange("p o k c -> p (o k c)"), ident[:])
                    mm.then_inc(xT_ps, 1)
                if runs(t, 2, NPAIR):
                    p = t - 2
                    pe.wait_ge(pT_bd, 16 * NB * (p + 1))
                    at_least(pe, h2_sb, p)
                    pe.wait_ge(v_lo, p + 1)
                    for g in range(2):
                        for h in range(H):
                            o = (g * H + h) * (HD + 1)
                            for n, (a, b) in enumerate(((0, 0), (1, 0), (0, 1))):
                                mm = pe.matmul(yp[:, o:o + HD + 1], p_bd[u][:, g, a, :, h], v_s[u][:, g, b, h, :],
                                               start=(g == 0 and h == 0 and n == 0), stop=(n == 2), skip_group_check=True)
                    mm.then_inc(pv_ps, 1)
                if runs(t, 0, NPAIR):
                    pe.wait_ge(xT_sb, t + 1)
                    at_least(pe, v_lo, t)
                    for g in range(2):
                        n = 0
                        for w in (tok_w_h, tok_w_l):
                            for half in range(2):
                                mm = pe.matmul(hv[:, g * D:(g + 1) * D], xT[:, g * P + half:g * P + half + P], w[:, half, :],
                                               start=(g == 0 and n == 0), stop=(n == 3), skip_group_check=True)
                                n += 1
                    mm.then_inc(tok_ps, 1)
                if runs(t, 1, NPAIR):
                    p = t - 1
                    w = 1 - u
                    pe.wait_ge(k_bd, 16 * (HA + HB) * (p + 1))
                    at_least(pe, sc_sb, p)
                    for g in range(2):
                        pe.matmul(sc[g][:, 0:H * TP], ident[:], causal[:].rearrange("p h s -> p (h s)"), start=True, stop=False,
                                  skip_group_check=True)
                    for g in range(2):
                        for a, b in ((0, 0), (1, 0), (0, 1)):
                            for c in range(NB):
                                r = slice(c * TP, (c + 1) * TP)
                                q = slice(g * P + c * TP, g * P + (c + 1) * TP)
                                pe.matmul(sc[g][r, 0:HA * TP], qk_s[w][:, 0, a, q], k_a[w][:, b, :, q], start=False, stop=False,
                                          skip_group_check=True)
                            for c in range(NB):
                                r = slice(c * TP, (c + 1) * TP)
                                q = slice(g * P + c * TP, g * P + (c + 1) * TP)
                                mm = pe.matmul(sc[g][r, HA * TP:H * TP], qk_s[w][0:R, 2, a, q], k_b[w][:, b, :, q],
                                               start=False, stop=(b == 1), skip_group_check=True)
                        mm.then_inc(sc_ps, 1)
                if runs(t, 2, NPAIR):
                    p = t - 2
                    pe.wait_ge(y_hi, p + 1)
                    pe.wait_ge(y_lo, p + 1)
                    at_least(pe, x2T_sb, p)
                    for g in range(2):
                        mm = turn(t1, y_s[:, g].rearrange("p k d -> p (k d)"), g * P)
                    mm.then_inc(yT_ps, 1)
                if runs(t, 0, NPAIR):
                    pe.wait_ge(xn_hi, t + 1)
                    pe.wait_ge(xn_lo, t + 1)
                    for g in range(2):
                        mm = turn(t0, xn_s[:, g].rearrange("p k d -> p (k d)"), g * P)
                    mm.then_inc(xnT_ps, 1)
                if runs(t, 2, NPAIR):
                    p = t - 2
                    pe.wait_ge(yT_sb, p + 1)
                    for g in range(2):
                        mm = rows_by_weights(yp[:, g * D:(g + 1) * D], yT, g * P, proj_h, proj_l, slice(0, D))
                    mm.then_inc(proj_ps, 1)
                if runs(t, 0, NPAIR):
                    pe.wait_ge(xnT_sb, t + 1)
                    at_least(pe, qk_lo, 2 * t)
                    for j in range(3):
                        dst = qk01[:, j * PW:(j + 1) * PW] if j < 2 else qk2[:, 0:PW]
                        for n, (k, w) in enumerate(parts(qkv_h, qkv_l)):
                            mm = pe.matmul(dst, w[:, j * P:(j + 1) * P], xnT[:, k, :], start=(n == 0), stop=(n == 4))
                        if j > 0:
                            mm.then_inc(qk_ps, 1)
                    for g in range(2):
                        mm = rows_by_weights(hv[:, g * D:(g + 1) * D], xnT, g * P, qkv_h, qkv_l, slice(2 * D, 3 * D))
                    mm.then_inc(v_ps, 1)
                if runs(t, 2, NPAIR):
                    p = t - 2
                    pe.wait_ge(x2_hi, p + 1)
                    pe.wait_ge(x2_lo, p + 1)
                    for g in range(2):
                        mm = turn(t1, x2_s[:, g].rearrange("p k d -> p (k d)"), g * P)
                    mm.then_inc(x2T_ps, 1)

            pipeline(pe, step, NPAIR, 2)

            pe.wait_ge(x2T_sb, NPAIR)
            pe.wait_ge(v_lo, NPAIR)
            for g in range(NG):
                for n, (k, w) in enumerate(parts(router_h, router_l)):
                    mm = pe.matmul(hv[:, g * E:(g + 1) * E], x2T[:, k, g * P:(g + 1) * P], w, start=(g == 0 and n == 0),
                                   stop=(n == 4), skip_group_check=True)
            mm.then_inc(logit_ps, 1)
            pe.wait_ge(router_d, 10 + E)

            def ffn_step(s, u):
                if runs(s, 0, NBLK):
                    for g in range(4):
                        mm = pe.transpose(t0[:, g // 2, (g % 2) * P:(g % 2 + 1) * P],
                                          onehot[:, ds(4 * s + g, 1), :].rearrange("p o c -> p (o c)"), ident[:])
                    mm.then_inc(ohT_ps, 1)
                    for j in range(4):
                        at_least(pe, gh_sb, 4 * s + j - 3 if not isinstance(s, int) or s > 0 else 0)
                        if j == 0:
                            pe.wait_ge(ohT_sb, s + 1)
                        pe.matmul(pre[j][:], lower[:, j, :], ohT[u][0:9, :], start=True, stop=False)
                        for n, (k, w) in enumerate(parts(w1_h, w1_l)):
                            mm = pe.matmul(pre[j][:], w[:, j * P:(j + 1) * P], x2T[:, k, ds(s * BW, BW)],
                                           start=False, stop=(n == 4))
                        mm.then_inc(pre_ps, 1)
                if runs(s, 1, NBLK):
                    q = s - 1
                    v = 1 - u
                    pe.wait_ge(gl_sb, 4 * q + 4)
                    at_least(pe, o_sb, q)
                    for g in range(4):
                        dst = ffn[g // 2][:, (g % 2) * D:(g % 2 + 1) * D]
                        c = slice(g * P, (g + 1) * P)
                        pe.matmul(dst, ohT[v][0:40, c], b2_parts[:], start=(g % 2 == 0), stop=False, skip_group_check=True)
                        for j in range(4):
                            pe.matmul(dst, g_h[v][:, j, c], w2_h[:, j, :], start=False, stop=False, skip_group_check=True)
                            pe.matmul(dst, g_l[v][:, j, c], w2_h[:, j, :], start=False, stop=False, skip_group_check=True)
                            mm = pe.matmul(dst, g_h[v][:, j, c], w2_l[:, j, :], start=False, stop=(j == 3), skip_group_check=True)
                        if g % 2:
                            mm.then_inc(ffn_ps, 1)

            pipeline(pe, ffn_step, NBLK, 1)


def kernel(x, L0_tok_W, L0_tok_b, L0_attn_W_attn, L0_attn_b_attn, L0_attn_W_proj, L0_attn_b_proj,
           L0_ffn_enc_w, L0_ffn_enc_b, L0_ffn_sw_w, L0_ffn_sw_b, L0_ffn_w1, L0_ffn_b1, L0_ffn_w2, L0_ffn_b2):
    import numpy as np
    import concourse.bacc as bacc
    from concourse.bass_utils import run_bass_kernel_spmd

    def stack(w):
        a = [w[0:64], w[64:128], w[128:192]]
        return np.stack([np.concatenate([a[0], a[1]]), np.concatenate([a[2], a[0]]), np.concatenate([a[1], a[2]])], axis=1)

    inputs = [np.asarray(v) for v in (x, L0_tok_W, L0_tok_b, L0_attn_W_attn, L0_attn_b_attn, L0_attn_W_proj, L0_attn_b_proj,
                                      L0_ffn_enc_w, L0_ffn_enc_b, L0_ffn_sw_w, L0_ffn_sw_b, L0_ffn_w1, L0_ffn_b1, L0_ffn_w2, L0_ffn_b2)]
    x, tok_W, tok_b, W_attn, b_attn, W_proj, b_proj, enc_w, enc_b, sw_w, sw_b, w1, b1, w2, b2 = inputs
    order = np.concatenate([np.arange(0, 128), np.arange(192, 320), np.arange(128, 192), np.arange(320, 384), np.arange(384, 576)])
    halves = [tok_W[:, 0:CH].T, tok_W[:, CH:].T]
    vb = b_attn[384:]
    arrays = {
        "x": x,
        "tok_w": np.stack([np.concatenate([w, w]) for w in halves], axis=1),
        "tok_b": tok_b[None, :],
        "qkv_w": stack(W_attn[:, order]),
        "qk_b": b_attn[order[:384]].reshape(3, P).T,
        "v_b": np.stack([vb[0:128], np.concatenate([vb[128:192], vb[128:192]])], axis=1),
        "proj_w": stack(W_proj),
        "proj_b": b_proj[None, :],
        "enc_wt": np.concatenate([stack(enc_w)[:, k].T[:, None] for k in range(3)], axis=1),
        "enc_b": enc_b[:, None],
        "sw_w": sw_w,
        "sw_b": sw_b[None, :],
        "w1": stack(w1.transpose(1, 0, 2).reshape(D, ER)),
        "b1": b1.reshape(4, P).T,
        "w2": w2.reshape(4, P, D).transpose(1, 0, 2),
        "b2": b2,
    }
    nc = bacc.Bacc("TRN2", target_bir_lowering=False, num_devices=1)
    feeds, args = {}, []
    for name, a in arrays.items():
        feeds[name + "_dram"] = np.ascontiguousarray(a)
        args.append(nc.dram_tensor(name + "_dram", a.shape, F32, kind="ExternalInput").ap())
    out = nc.dram_tensor("out_dram", (B, T, D), F32, kind="ExternalOutput").ap()
    audio_tower(nc, *args, out)
    result = run_bass_kernel_spmd(nc, [feeds], core_ids=[0])
    return result.results[0]["out_dram"]
```

```python
from contextlib import ExitStack

import concourse.bass as bass
from concourse import mybir

F32 = mybir.dt.float32
F16 = mybir.dt.float16
BF16 = mybir.dt.bfloat16
ALU = mybir.AluOpType
ACT = mybir.ActivationFunctionType
AX_X = mybir.AxisListType.X
ds = bass.ds

P = 128
B, T_IN, C_IN = 128, 256, 8
STRIDE = 8
CH = STRIDE * C_IN
T = T_IN // STRIDE - 1
TP = 32
D = 192
H, HD = 12, 16
HA, HB = 8, 4
NB = P // TP
NG = B // NB
NPAIR = NG // 2
NBLK = NG // 4
E, R = 8, 64
ER = E * R
WS = 64.0
EPS = 1e-5
MASKED = -1e30
OFF = 32768.0 * WS
PW = 2 * P
BW = 4 * P
FIRST = D + 7
LATER = 1168


def audio_tower(nc, x, tok_w, first_rows, qkv_w, proj_w, later_rows, w1, w2, out):
    x_rows = x.rearrange("b (c t) f -> (b c) (t f)", t=STRIDE).rearrange("(g p) f -> p g f", p=P)

    with ExitStack() as ctx:
        def sb(name, shape, dt=F32):
            return ctx.enter_context(nc.sbuf_tensor(name, shape, dt))

        def sem(name):
            return ctx.enter_context(nc.semaphore(name))

        tok_w_f = sb("tok_w_f", [P, 2, D])
        qkv_w_f = sb("qkv_w_f", [P, 3, 3 * D])
        proj_w_f = sb("proj_w_f", [P, 3, D])
        w1_f = sb("w1_f", [P, 3, ER])
        w2_f = sb("w2_f", [P, 4, D])
        first_f = sb("first_f", [P, FIRST])
        tok_b = first_f[:, 0:D]
        qk_b_f = first_f[:, D:D + 3]
        b1_f = first_f[:, D + 3:D + 7]
        later_f = sb("later_f", [P, LATER])
        proj_b = later_f[:, 0:D]
        sw_b = later_f[:, D:D + E]
        v_b_wide = later_f[:, 200:456].rearrange("p (k c) -> p k c", k=2)
        enc_b_wide = later_f[0:R, 456:584]
        sw_w_f = later_f[0:R, 584:592]
        enc_wt_f = later_f[0:R, 592:976].rearrange("p (k c) -> p k c", k=3)
        b2_f = later_f[0:40, 976:1168]
        qk_b_s = sb("qk_b_s", [P, 3])
        tok_w_h = sb("tok_w_h", [P, 2, D], F16)
        tok_w_l = sb("tok_w_l", [P, 2, D], F16)
        qkv_h = sb("qkv_h", [P, 3, 3 * D], F16)
        qkv_l = sb("qkv_l", [P, 2, 3 * D], F16)
        proj_h = sb("proj_h", [P, 3, D], F16)
        proj_l = sb("proj_l", [P, 2, D], F16)
        w1_h = sb("w1_h", [P, 3, ER], F16)
        w1_l = sb("w1_l", [P, 2, ER], F16)
        w2_h = sb("w2_h", [P, 4, D], F16)
        w2_l = sb("w2_l", [P, 4, D], F16)
        router_f = sb("router_f", [P, 3, E])
        router_h = sb("router_h", [P, 3, E], F16)
        router_l = sb("router_l", [P, 2, E], F16)
        b2_h = sb("b2_h", [40, D], F16)
        b2_parts = sb("b2_parts", [40, D], F16)
        out_b = sb("out_b", [P, D])
        route_b = sb("route_b", [P, E])
        ident = sb("ident", [P, P], F16)
        causal = sb("causal", [P, H, TP], BF16)
        lower = sb("lower", [9, 4, P], BF16)
        pick = sb("pick", [P, E])
        x_f = sb("x_f", [P, NG, CH])
        x_s = sb("x_s", [P, NG, 2, CH], F16)
        xT = sb("xT", [P, PW + 1], F16)
        h_all = sb("h_all", [P, NPAIR, 2, D])
        stats = sb("stats", [P, 2, 2, 6])
        mv = sb("mv", [P, 2, 2, 2])
        var_eps = sb("var_eps", [P, 2, 2])
        half = sb("half", [P, 2])
        rstd = sb("rstd", [P, 2, 2])
        xn_f = sb("xn_f", [P, 2, D])
        xn_s = sb("xn_s", [P, 2, 2, D], F16)
        xnT = sb("xnT", [P, 3, PW], F16)
        qk_s = [sb(f"qk_s{u}", [P, 3, 2, PW], F16) for u in range(2)]
        v_s = [sb(f"v_s{u}", [P, 2, 2, H, HD + 1], F16) for u in range(2)]
        k_a = [sb(f"k_a{u}", [P, 2, HA, PW], F16) for u in range(2)]
        k_b = [sb(f"k_b{u}", [HB * HD, 2, HB, PW], F16) for u in range(2)]
        top = sb("top", [P, 2, H])
        scores = sb("scores", [P, 2, H, TP])
        prob = sb("prob", [P, 2, H, TP])
        probT = sb("probT", [P, 2, TP, H])
        probT_s = sb("probT_s", [P, 2, 2, TP, H], F16)
        p_mem = [sb(f"p_mem{u}", [P, 4 * P * H], F16) for u in range(2)]
        p_bd = [m[:].rearrange("p (g k c h) -> p g k c h", g=2, k=2, h=H) for m in p_mem]
        rden = sb("rden", [P, 2, H])
        y_f = sb("y_f", [P, 2, H, HD])
        y_s = sb("y_s", [P, 2, 2, D], F16)
        yT = sb("yT", [P, 3, PW], F16)
        h = sb("h", [P, 2, D])
        spacer = sb("spacer", [P, 1])
        x2_f = sb("x2_f", [P, 2, D])
        x2_s = sb("x2_s", [P, 2, 2, D], F16)
        x2T = sb("x2T", [P, 3, NG * P], F16)
        logit = sb("logit", [P, NG, E])
        l_top = sb("l_top", [P, NG])
        l_exp = sb("l_exp", [P, NG, E])
        l_sum = sb("l_sum", [P, NG])
        p_top = sb("p_top", [P, NG])
        cand = sb("cand", [P, NG, E])
        c_top = sb("c_top", [P, NG])
        onehot = x_s[:].rearrange("p g k c -> p g (k c)")
        ohT = [sb(f"ohT{u}", [64, BW], F16) for u in range(2)]
        g_f = [x_f[:].rearrange("p g c -> p (g c)")[:, u * BW:(u + 1) * BW] for u in range(2)]
        g_h = [m[:, 0:4 * BW].rearrange("p (j c) -> p j c", j=4) for m in p_mem]
        g_l = [m[:, 4 * BW:8 * BW].rearrange("p (j c) -> p j c", j=4) for m in p_mem]
        o_f = [m[:, 8 * BW:8 * BW + 8 * D].bitcast(F32).rearrange("p (g d) -> p g d", g=4) for m in p_mem]

        bank = [ctx.enter_context(nc.psum_tensor(f"bank{i}", [P, 512], F32)) for i in range(8)]
        t0 = bank[0][:].bitcast(F16).rearrange("p (k c) -> p k c", k=4)
        t1 = bank[1][:].bitcast(F16).rearrange("p (k c) -> p k c", k=4)
        hv = bank[2]
        yp = bank[3]
        qk01, qk2 = bank[4], bank[5]
        sc = [bank[6], bank[7]]
        pre = [bank[2], bank[3], bank[4], bank[5]]
        ffn = [bank[6], bank[7]]

        w_load = {n: sem(f"{n}_load") for n in ("tok", "first", "qkv", "later", "ffn")}
        x_load = [sem(f"x_load{i}") for i in range(4)]
        consts = sem("consts")
        zeroed = sem("zeroed")
        zeroed_d = sem("zeroed_d")
        zeroed_x = sem("zeroed_x")
        folded, folded_d = sem("folded"), sem("folded_d")
        split_a = sem("split_a")
        split_d = sem("split_d")
        x_hi = sem("x_hi")
        x_lo = sem("x_lo")
        xT_ps, xT_sb = sem("xT_ps"), sem("xT_sb")
        tok_ps, h_sb = sem("tok_ps"), sem("h_sb")
        bn1, ag1, rs1, xn_sb, xn_hi, xn_lo = (sem(n) for n in ("bn1", "ag1", "rs1", "xn_sb", "xn_hi", "xn_lo"))
        ve1, ve2 = sem("ve1"), sem("ve2")
        xnT_ps, xnT_sb = sem("xnT_ps"), sem("xnT_sb")
        qk_ps, qk_hi, qk_lo = sem("qk_ps"), sem("qk_hi"), sem("qk_lo")
        v_ps, v_hi, v_lo = sem("v_ps"), sem("v_hi"), sem("v_lo")
        k_bd = [sem(f"k_bd{u}") for u in range(2)]
        sc_ps, sc_top, sc_sb = sem("sc_ps"), sem("sc_top"), sem("sc_sb")
        pr_sb, pT_sb, pT_hi, pT_lo, pT_bd = (sem(n) for n in ("pr_sb", "pT_sb", "pT_hi", "pT_lo", "pT_bd"))
        pv_ps, rden_sb, y_sb, y_hi, y_lo = (sem(n) for n in ("pv_ps", "rden_sb", "y_sb", "y_hi", "y_lo"))
        yT_ps, yT_sb = sem("yT_ps"), sem("yT_sb")
        hb_sb, proj_ps, h2_sb = sem("hb_sb"), sem("proj_ps"), sem("h2_sb")
        bn2, ag2, rs2, x2_sb, x2_hi, x2_lo = (sem(n) for n in ("bn2", "ag2", "rs2", "x2_sb", "x2_hi", "x2_lo"))
        x2T_ps, x2T_sb = sem("x2T_ps"), sem("x2T_sb")
        logit_ps, router_d, router_a = sem("logit_ps"), sem("router_d"), sem("router_a")
        ohT_ps, ohT_sb = sem("ohT_ps"), sem("ohT_sb")
        pre_ps, g_sb, gh_sb, gl_sb = sem("pre_ps"), sem("g_sb"), sem("gh_sb"), sem("gl_sb")
        ffn_ps, o_sb, stored = sem("ffn_ps"), sem("o_sb"), sem("stored")

        X_CUTS = [0, 2, 8, 16, NG]

        def at_least(eng, s, n):
            if not isinstance(n, int) or n > 0:
                eng.wait_ge(s, n)

        def pipeline(eng, step, n, ahead, first, last):
            for t in range(first):
                step(t, t % 2, t // 2)
            with eng.Fori(first // 2, last // 2) as i:
                for u in range(2):
                    step(2 * i + u, u, i)
            for t in range(last, n + ahead):
                step(t, t % 2, t // 2)

        STAGES = 6

        def attention(eng, step):
            pipeline(eng, step, NPAIR, STAGES - 1, STAGES, NPAIR - 2)

        def has(t, lag):
            return not isinstance(t, int) or 0 <= t - lag < NPAIR

        block = ctx.enter_context(nc.Block())

        @block.sync
        def _(sp):
            sp.dma_start(x_f[:, 0:2, :], x_rows[:, 0:2, :]).then_inc(x_load[0], 16)
            sp.dma_start(tok_w_f[:], tok_w).then_inc(w_load["tok"], 16)
            sp.dma_start(first_f[:], first_rows).then_inc(w_load["first"], 16)
            sp.dma_start(x_f[:, 2:8, :], x_rows[:, 2:8, :]).then_inc(x_load[1], 16)
            sp.dma_start(qkv_w_f[:], qkv_w).then_inc(w_load["qkv"], 16)
            sp.dma_start(proj_w_f[:], proj_w).then_inc(w_load["later"], 16)
            sp.dma_start(later_f[:], later_rows).then_inc(w_load["later"], 16)
            for i in range(2, 4):
                a, b = X_CUTS[i], X_CUTS[i + 1]
                sp.dma_start(x_f[:, a:b, :], x_rows[:, a:b, :]).then_inc(x_load[i], 16)
            sp.dma_start(w1_f[:], w1).then_inc(w_load["ffn"], 16)
            sp.dma_start(w2_f[:], w2).then_inc(w_load["ffn"], 16)

            def step(t, u, i):
                if has(t, 1):
                    sp.wait_ge(qk_hi, 2 * t)
                    sp.wait_ge(qk_lo, 2 * t)
                    for h in range(HA):
                        r = slice(h * HD, (h + 1) * HD)
                        sp.dma_start(k_a[1 - u][r, :, h, :], qk_s[1 - u][r, 1, :, :]).then_inc(k_bd[1 - u], 16)
                    for h in range(HB):
                        r = slice(h * HD, (h + 1) * HD)
                        s = slice(R + h * HD, R + (h + 1) * HD)
                        sp.dma_start(k_b[1 - u][r, :, h, :], qk_s[1 - u][s, 2, :, :]).then_inc(k_bd[1 - u], 16)
                if has(t, 2):
                    sp.wait_ge(pT_hi, t - 1)
                    sp.wait_ge(pT_lo, t - 1)
                    for b in range(NB):
                        r = slice(b * TP, (b + 1) * TP)
                        sp.dma_start(p_bd[u][r, :, :, r, :], probT_s[r]).then_inc(pT_bd, 16)

            sp.wait_ge(zeroed, 2)
            sp.wait_ge(zeroed_d, 1)
            attention(sp, step)

            for s in range(NBLK):
                sp.wait_ge(o_sb, s + 1)
                at_least(sp, stored, 16 * NB * s)
                for b in range(NB):
                    dst = out.rearrange("(s g b) t d -> s b t g d", g=4, b=NB)[s, b]
                    sp.dma_start(dst, o_f[s % 2][b * TP:b * TP + T, :, :]).then_inc(stored, 16)
            sp.wait_ge(stored, 16 * NB * NBLK)

        @block.gpsimd
        def _(pool):
            made = [0]

            def make(ins):
                ins.then_inc(consts, 1)
                made[0] += 1
                pool.wait_ge(consts, made[0])

            make(pool.memset(half[:], -0.5))
            make(pool.memset(ident[:], 0.0))
            make(pool.affine_select(out=ident[:], in_=ident[:], compare_op=ALU.not_equal, fill=1.0, base=0,
                                    pattern=[[-1, P]], channel_multiplier=1))
            make(pool.memset(causal[:], 0.0))
            for b in range(NB):
                r = slice(b * TP, (b + 1) * TP)
                make(pool.affine_select(out=causal[r], in_=causal[r], compare_op=ALU.is_ge, fill=MASKED, base=0,
                                        pattern=[[0, H], [-1, TP]], channel_multiplier=1))
            make(pool.memset(lower[:], -OFF))
            make(pool.memset(lower[0:E], 0.0))
            lower_e = lower[0:E].rearrange("e j (k c) -> e j k c", k=2)
            make(pool.affine_select(out=lower_e, in_=lower_e, compare_op=ALU.not_equal, fill=OFF, base=0,
                                    pattern=[[-2, 4], [-1, 2], [0, R]], channel_multiplier=1))
            for u in range(2):
                pool.memset(p_mem[u][:].bitcast(F32), 0.0).then_inc(zeroed, 1)

            def step(t, u, i):
                if has(t, 0):
                    pool.wait_ge(ve1, t + 1)
                    pool.tensor_tensor(rstd[:, 0, :], var_eps[:, 0, :], half[:], ALU.pow).then_inc(rs1, 1)
                    pool.wait_ge(xn_hi, t + 1)
                    pool.tensor_tensor(xn_s[:, :, 1, :], xn_f[:], xn_s[:, :, 0, :], ALU.subtract).then_inc(xn_lo, 1)
                    if isinstance(t, int) and t == 0:
                        pool.wait_ge(folded, 3)
                    pool.tensor_tensor(h_all[:, t], h[:], out_b[:].unsqueeze(1).to_broadcast([P, 2, D]),
                                       ALU.add).then_inc(hb_sb, 1)
                if has(t, 4):
                    pool.wait_ge(ve2, t - 3)
                    pool.tensor_tensor(rstd[:, 1, :], var_eps[:, 1, :], half[:], ALU.pow).then_inc(rs2, 1)
                if has(t, 2):
                    pool.wait_ge(pT_hi, t - 1)
                    pool.tensor_tensor(probT_s[:, :, 1], probT[:], probT_s[:, :, 0], ALU.subtract).then_inc(pT_lo, 1)
                if has(t, 4):
                    pool.wait_ge(x2_hi, t - 3)
                    pool.tensor_tensor(x2_s[:, :, 1, :], x2_f[:], x2_s[:, :, 0, :], ALU.subtract).then_inc(x2_lo, 1)
                if has(t, 3):
                    pool.wait_ge(y_hi, t - 2)
                    pool.tensor_tensor(y_s[:, :, 1, :], y_f[:].rearrange("p g h d -> p g (h d)"), y_s[:, :, 0, :],
                                       ALU.subtract).then_inc(y_lo, 1)

            attention(pool, step)

        @block.scalar
        def _(act):
            def hi(dst, src):
                return act.activation(dst, src, ACT.Copy, scale=WS)

            def x_part(i):
                a, b = X_CUTS[i], X_CUTS[i + 1]
                act.wait_ge(x_load[i], 16)
                act.copy(x_s[:, a:b, 0, :], x_f[:, a:b, :]).then_inc(x_hi, 1)

            def setup(t):
                if t == 0:
                    x_part(0)
                    act.wait_ge(w_load["tok"], 16)
                    hi(tok_w_h[:], tok_w_f[:]).then_inc(split_a, 1)
                    x_part(1)
                    act.wait_ge(w_load["first"], 16)
                    hi(qk_b_s[:], qk_b_f).then_inc(split_a, 1)
                    act.wait_ge(w_load["qkv"], 16)
                    hi(qkv_h[:], qkv_w_f[:]).then_inc(split_a, 1)
                if t == 1:
                    act.wait_ge(w_load["later"], 32)
                    hi(proj_h[:], proj_w_f[:]).then_inc(split_a, 1)
                    x_part(2)
                    x_part(3)
                if t == 2:
                    hi(b2_h[0:E], b2_f[0:E])
                    hi(b2_h[32:32 + E], b2_f[32:32 + E]).then_inc(split_a, 1)
                    act.wait_ge(w_load["ffn"], 32)
                    hi(w1_h[:], w1_f[:]).then_inc(split_a, 1)
                if t == 3:
                    hi(w2_h[:], w2_f[:]).then_inc(split_a, 1)
                    act.wait_ge(folded, 3)
                    hi(router_h[:], router_f[:]).then_inc(split_a, 1)

            def x_turned(t):
                act.wait_ge(xT_ps, t + 1)
                at_least(act, tok_ps, t)
                act.copy(xT[:, 0:PW].rearrange("p (g c) -> p g c", g=2),
                         t0[:, 3:4, :].rearrange("p o (g c) -> p (o g) c", g=2)).then_inc(xT_sb, 1)

            def step(t, u, i):
                if isinstance(t, int):
                    setup(t)
                if isinstance(t, int) and t == 0:
                    x_turned(0)
                if has(t, 1):
                    w = 1 - u
                    act.wait_ge(qk_ps, 2 * t - 1)
                    for j in range(2):
                        mm = act.activation(qk_s[w][:, j, 0, :], qk01[:, j * PW:(j + 1) * PW], ACT.Identity,
                                            bias=qk_b_s[:, j:j + 1])
                    mm.then_inc(qk_hi, 1)
                    act.wait_ge(qk_ps, 2 * t)
                    act.activation(qk_s[w][:, 2, 0, :], qk2[:, 0:PW], ACT.Identity, bias=qk_b_s[:, 2:3]).then_inc(qk_hi, 1)
                if has(t, -1):
                    x_turned(t + 1)
                if has(t, 5):
                    act.wait_ge(x2T_ps, t - 4)
                    act.copy(x2T[:, :, ds((t - 5) * PW, PW)], t1[:, 0:3, :]).then_inc(x2T_sb, 1)
                if has(t, 4):
                    act.wait_ge(yT_ps, t - 3)
                    at_least(act, proj_ps, t - 4)
                    act.copy(yT[:], t1[:, 0:3, :]).then_inc(yT_sb, 1)
                if has(t, 0):
                    act.wait_ge(xn_sb, t + 1)
                    at_least(act, xnT_ps, t)
                    act.copy(xn_s[:, :, 0, :], xn_f[:]).then_inc(xn_hi, 1)
                if has(t, 2):
                    act.wait_ge(sc_sb, t - 1)
                    at_least(act, pT_sb, t - 2)
                    act.activation(prob[:], scores[:], ACT.Exp, scale=0.25 / (WS * WS)).then_inc(pr_sb, 1)
                if has(t, 0):
                    act.wait_ge(xnT_ps, t + 1)
                    at_least(act, v_ps, t)
                    act.copy(xnT[:], t0[:, 0:3, :]).then_inc(xnT_sb, 1)
                if has(t, 1):
                    act.wait_ge(v_ps, t)
                    at_least(act, pv_ps, t - 2)
                    act.copy(v_s[1 - u][:, :, 0, :, 0:HD],
                             hv[:, 0:2 * D].rearrange("p (g h d) -> p g h d", g=2, h=H)).then_inc(v_hi, 1)
                if has(t, 2):
                    act.wait_ge(pT_sb, t - 1)
                    at_least(act, pT_bd, 16 * NB * (t - 2))
                    act.copy(probT_s[:, :, 0], probT[:]).then_inc(pT_hi, 1)
                if has(t, 4):
                    act.wait_ge(x2_sb, t - 3)
                    at_least(act, x2T_ps, t - 4)
                    act.copy(x2_s[:, :, 0, :], x2_f[:]).then_inc(x2_hi, 1)
                if has(t, 3):
                    act.wait_ge(y_sb, t - 2)
                    at_least(act, yT_ps, t - 3)
                    act.copy(y_s[:, :, 0, :], y_f[:].rearrange("p g h d -> p g (h d)")).then_inc(y_hi, 1)

            attention(act, step)

            act.wait_ge(router_d, 3)
            act.activation(l_exp[:], l_exp[:], ACT.Exp).then_inc(router_a, 1)

            def ffn_step(s, u, i):
                if not isinstance(s, int) or s < NBLK:
                    act.wait_ge(ohT_ps, s + 1)
                    act.copy(ohT[u][:], t0[0:64, 0:2, :].rearrange("p k c -> p (k c)")).then_inc(ohT_sb, 1)
                    for j in range(4):
                        act.wait_ge(pre_ps, 4 * s + j + 1)
                        at_least(act, gl_sb, 4 * s + j - 1)
                        act.activation(g_f[j % 2], pre[j][:], ACT.Gelu, bias=b1_f[:, j:j + 1], scale=1.0 / WS).then_inc(g_sb, 1)
                        act.activation(g_h[u][:, j, :], pre[j][:], ACT.Gelu, bias=b1_f[:, j:j + 1],
                                       scale=1.0 / WS).then_inc(gh_sb, 1)

            pipeline(act, ffn_step, NBLK, 1, 4, NBLK)

        @block.vector
        def _(dve):
            def lo(dst, src, high):
                return dve.scalar_tensor_tensor(out=dst, in0=src, scalar=WS, in1=high, op0=ALU.mult, op1=ALU.subtract)

            def x_part(i):
                a, b = X_CUTS[i], X_CUTS[i + 1]
                dve.wait_ge(x_hi, i + 1)
                dve.tensor_tensor(x_s[:, a:b, 1, :], x_f[:, a:b, :], x_s[:, a:b, 0, :], ALU.subtract).then_inc(x_lo, 1)

            def setup(t):
                if t == 0:
                    dve.memset(xT[:, PW:PW + 1], 0.0).then_inc(zeroed_x, 1)
                    x_part(0)
                    dve.wait_ge(split_a, 1)
                    lo(tok_w_l[:], tok_w_f[:], tok_w_h[:]).then_inc(split_d, 1)
                    for u in range(2):
                        dve.memset(v_s[u][:, :, 0, :, HD:HD + 1], WS)
                        dve.memset(v_s[u][:, :, 1, :, HD:HD + 1], 0.0)
                    dve.memset(b2_parts[:], 0.0)
                    for u in range(2):
                        dve.memset(k_b[u][:].bitcast(F32), 0.0)
                        mm = dve.memset(k_a[u][:].bitcast(F32), 0.0)
                    mm.then_inc(zeroed_d, 1)
                if t == 1:
                    x_part(1)
                    dve.wait_ge(split_a, 3)
                    lo(qkv_l[:], qkv_w_f[:, 0:2, :], qkv_h[:, 0:2, :]).then_inc(split_d, 1)
                    dve.wait_ge(folded, 1)
                    dve.tensor_copy(router_f[:], sc[0][:, 0:3 * E].rearrange("p (k e) -> p k e", k=3)).then_inc(folded_d, 1)
                    dve.tensor_tensor(out_b[:], sc[1][:, 0:D], proj_b, ALU.add).then_inc(folded, 1)
                    dve.tensor_tensor(route_b[:], sc[1][:, D:D + E], sw_b, ALU.add).then_inc(folded, 1)
                if t == 2:
                    x_part(2)
                    x_part(3)
                    dve.wait_ge(split_a, 4)
                    lo(proj_l[:], proj_w_f[:, 0:2, :], proj_h[:, 0:2, :]).then_inc(split_d, 1)
                if t == 4:
                    dve.wait_ge(split_a, 8)
                    dve.wait_ge(zeroed_d, 1)
                    dve.tensor_copy(b2_parts[0:E], b2_h[0:E]).then_inc(split_d, 1)
                    lo(b2_parts[32:32 + E], b2_f[32:32 + E], b2_h[32:32 + E]).then_inc(split_d, 1)
                    lo(router_l[:], router_f[:, 0:2, :], router_h[:, 0:2, :]).then_inc(split_d, 1)
                    lo(w1_l[:], w1_f[:, 0:2, :], w1_h[:, 0:2, :]).then_inc(split_d, 1)
                if t == 5:
                    lo(w2_l[:], w2_f[:], w2_h[:]).then_inc(split_d, 1)

            def spread(p, k, rows, bn, ag, ve):
                for g in range(2):
                    dve.bn_stats(stats[:, k, g, :], rows[:, g, :]).then_inc(bn, 1)
                dve.wait_ge(bn, 2 * p + 2)
                dve.memset(spacer[:], 0.0)
                for g in range(2):
                    dve.bn_aggr(mv[:, k, g, :], stats[:, k, g, :]).then_inc(ag, 1)
                dve.wait_ge(ag, 2 * p + 2)
                dve.tensor_scalar(var_eps[:, k, :], mv[:, k, :, 1], EPS, None, ALU.add).then_inc(ve, 1)

            def centre(p, k, rows, dst, rs, done):
                dve.wait_ge(rs, p + 1)
                for g in range(2):
                    mm = dve.tensor_scalar(dst[:, g, :], rows[:, g, :], mv[:, k, g, 0:1], rstd[:, k, g:g + 1],
                                           ALU.subtract, ALU.mult)
                mm.then_inc(done, 1)

            def scores_top(p, g):
                s = sc[g][:, 0:H * TP].rearrange("p (h s) -> p h s", h=H)
                dve.wait_ge(sc_ps, 2 * p + g + 1)
                dve.tensor_reduce(top[:, g, :], s, AX_X, ALU.max).then_inc(sc_top, 1)

            def scores_less_top(p, g):
                s = sc[g][:, 0:H * TP].rearrange("p (h s) -> p h s", h=H)
                dve.wait_ge(sc_top, 2 * p + g + 1)
                if g == 0:
                    at_least(dve, pr_sb, p)
                mm = dve.tensor_tensor(scores[:, g], s, top[:, g, :].unsqueeze(2).to_broadcast([P, H, TP]),
                                       ALU.subtract)
                if g == 1:
                    mm.then_inc(sc_sb, 1)

            def step(t, u, i):
                if isinstance(t, int):
                    setup(t)
                if has(t, 0):
                    dve.wait_ge(tok_ps, t + 1)
                    if isinstance(t, int) and t == 0:
                        dve.wait_ge(w_load["first"], 16)
                    at_least(dve, hb_sb, t)
                    dve.scalar_tensor_tensor(out=h[:], in0=hv[:, 0:2 * D].rearrange("p (g d) -> p g d", g=2),
                                             scalar=1.0 / WS, in1=tok_b.unsqueeze(1).to_broadcast([P, 2, D]),
                                             op0=ALU.mult, op1=ALU.add).then_inc(h_sb, 1)
                    dve.wait_ge(h_sb, t + 1)
                    spread(t, 0, h, bn1, ag1, ve1)
                if has(t, 1):
                    w = 1 - u
                    for j in range(3):
                        if j != 1:
                            dve.wait_ge(qk_hi, 2 * t - 1 + j // 2)
                        src = qk01[:, j * PW:(j + 1) * PW] if j < 2 else qk2[:, 0:PW]
                        mm = dve.scalar_tensor_tensor(out=qk_s[w][:, j, 1, :], in0=src, scalar=qk_b_s[:, j:j + 1],
                                                      in1=qk_s[w][:, j, 0, :], op0=ALU.add, op1=ALU.subtract)
                        if j > 0:
                            mm.then_inc(qk_lo, 1)
                if has(t, 2):
                    scores_top(t - 2, 0)
                if has(t, 0):
                    at_least(dve, xn_hi, t)
                    at_least(dve, xn_lo, t)
                    centre(t, 0, h, xn_f, rs1, xn_sb)
                if has(t, 2):
                    scores_less_top(t - 2, 0)
                    scores_top(t - 2, 1)
                    scores_less_top(t - 2, 1)
                if has(t, 4):
                    p = t - 4
                    dve.wait_ge(proj_ps, p + 1)
                    dve.wait_ge(hb_sb, p + 1)
                    dve.scalar_tensor_tensor(out=h_all[:, p], in0=yp[:, 0:2 * D].rearrange("p (g d) -> p g d", g=2),
                                             scalar=1.0 / WS, in1=h_all[:, p], op0=ALU.mult, op1=ALU.add).then_inc(h2_sb, 1)
                    dve.wait_ge(h2_sb, p + 1)
                    dve.memset(spacer[:], 0.0)
                    spread(p, 1, h_all[:, p], bn2, ag2, ve2)
                if has(t, 2):
                    p = t - 2
                    dve.wait_ge(pr_sb, p + 1)
                    at_least(dve, pT_hi, p)
                    at_least(dve, pT_lo, p)
                    dve.transpose(probT[:].rearrange("p g t h -> p g h t"), prob[:]).then_inc(pT_sb, 1)
                if has(t, 3):
                    p = t - 3
                    dve.wait_ge(pv_ps, p + 1)
                    yv = yp[:, 0:2 * H * (HD + 1)].rearrange("p (g h d) -> p g h d", g=2, h=H)
                    dve.reciprocal(rden[:], yv[:, :, :, HD]).then_inc(rden_sb, 1)
                    dve.wait_ge(rden_sb, p + 1)
                    at_least(dve, y_hi, p)
                    at_least(dve, y_lo, p)
                    dve.tensor_tensor(y_f[:], yv[:, :, :, 0:HD], rden[:].unsqueeze(3).to_broadcast([P, 2, H, HD]),
                                      ALU.mult).then_inc(y_sb, 1)
                if has(t, 1):
                    dve.wait_ge(v_hi, t)
                    dve.tensor_tensor(v_s[1 - u][:, :, 1, :, 0:HD], hv[:, 0:2 * D].rearrange("p (g h d) -> p g h d", g=2, h=H),
                                      v_s[1 - u][:, :, 0, :, 0:HD], ALU.subtract).then_inc(v_lo, 1)
                if has(t, 4):
                    p = t - 4
                    at_least(dve, x2_hi, p)
                    at_least(dve, x2_lo, p)
                    centre(p, 1, h_all[:, p], x2_f, rs2, x2_sb)

            attention(dve, step)

            dve.wait_ge(logit_ps, 1)
            dve.scalar_tensor_tensor(out=logit[:], in0=hv[:, 0:NG * E].rearrange("p (g e) -> p g e", e=E), scalar=1.0 / WS,
                                     in1=route_b[:].unsqueeze(1).to_broadcast([P, NG, E]),
                                     op0=ALU.mult, op1=ALU.add).then_inc(router_d, 1)
            dve.wait_ge(router_d, 1)
            dve.tensor_reduce(l_top[:], logit[:], AX_X, ALU.max).then_inc(router_d, 1)
            dve.wait_ge(router_d, 2)
            l_top_w = l_top[:].unsqueeze(2).to_broadcast([P, NG, E])
            dve.tensor_tensor(l_exp[:], logit[:], l_top_w, ALU.subtract).then_inc(router_d, 1)
            dve.tensor_tensor(cand[:], logit[:], l_top_w, ALU.is_equal).then_inc(router_d, 1)
            dve.memset(onehot, 0.0).then_inc(router_d, 1)
            for e in range(E):
                dve.memset(pick[:, e:e + 1], float(E - e)).then_inc(router_d, 1)
            dve.wait_ge(router_d, 5 + E)
            dve.tensor_tensor(cand[:], cand[:], pick[:].unsqueeze(1).to_broadcast([P, NG, E]), ALU.mult).then_inc(router_d, 1)
            dve.wait_ge(router_d, 6 + E)
            dve.tensor_reduce(c_top[:], cand[:], AX_X, ALU.max).then_inc(router_d, 1)
            dve.wait_ge(router_d, 7 + E)
            for c in (0, 32):
                dve.tensor_tensor(onehot[:, :, c:c + E], cand[:], c_top[:].unsqueeze(2).to_broadcast([P, NG, E]),
                                  ALU.is_equal).then_inc(router_d, 1)
            dve.memset(onehot[:, :, E:E + 1], 1.0).then_inc(router_d, 1)
            dve.wait_ge(router_a, 1)
            dve.tensor_reduce(l_sum[:], l_exp[:], AX_X, ALU.add).then_inc(router_d, 1)
            dve.wait_ge(router_d, 11 + E)
            dve.reciprocal(l_top[:], l_sum[:]).then_inc(router_d, 1)
            dve.wait_ge(router_d, 12 + E)
            dve.tensor_scalar(p_top[:], l_top[:], 1.0 / WS, None, ALU.mult).then_inc(router_d, 1)
            dve.wait_ge(router_d, 13 + E)

            def ffn_step(s, u, i):
                if not isinstance(s, int) or s < NBLK:
                    for j in range(4):
                        dve.wait_ge(gh_sb, 4 * s + j + 1)
                        dve.tensor_tensor(g_l[u][:, j, :], g_f[j % 2], g_h[u][:, j, :], ALU.subtract).then_inc(gl_sb, 1)
                if not isinstance(s, int) or s >= 1:
                    q = s - 1
                    at_least(dve, stored, 16 * NB * (q - 1))
                    for g in range(4):
                        if g % 2 == 0:
                            dve.wait_ge(ffn_ps, 2 * q + g // 2 + 1)
                        mm = dve.scalar_tensor_tensor(out=o_f[1 - u][:, g, :], in0=ffn[g // 2][:, (g % 2) * D:(g % 2 + 1) * D],
                                                      scalar=p_top[:, ds(4 * q + g, 1)], in1=h_all[:, ds(2 * q + g // 2, 1), g % 2, :].rearrange("p o d -> p (o d)"),
                                                      op0=ALU.mult, op1=ALU.add)
                    mm.then_inc(o_sb, 1)

            pipeline(dve, ffn_step, NBLK, 1, 4, NBLK)

        @block.tensor
        def _(pe):
            def parts(w_h, w_l):
                return [(0, w_h[:, 0]), (1, w_h[:, 1]), (2, w_h[:, 2]), (0, w_l[:, 0]), (1, w_l[:, 1])]

            def rows_by_weights(dst, actT, c0, w_h, w_l, cols):
                five = parts(w_h, w_l)
                for n, (k, w) in enumerate(five):
                    mm = pe.matmul(dst, actT[:, k, c0:c0 + P], w[:, cols], start=(n == 0), stop=(n == 4))
                return mm

            def turn(bank_t, src, c0):
                for k in range(3):
                    mm = pe.transpose(bank_t[:, k, c0:c0 + P], src[:, k * P:(k + 1) * P], ident[:])
                return mm

            def fold():
                pe.wait_ge(w_load["later"], 32)
                for k in range(3):
                    pe.matmul(sc[0][:, k * E:(k + 1) * E], enc_wt_f[:, k, :], sw_w_f, start=(k == 0), stop=True,
                              skip_group_check=True)
                pe.matmul(sc[1][:, 0:D], v_b_wide[:, 0, :], proj_w_f[:, 0, :], start=True, stop=False, skip_group_check=True)
                pe.matmul(sc[1][:, 0:D], v_b_wide[0:R, 1, :], proj_w_f[0:R, 1, :], start=False, stop=True, skip_group_check=True)
                pe.matmul(sc[1][:, D:D + E], enc_b_wide, sw_w_f, start=False, stop=True,
                          skip_group_check=True).then_inc(folded, 1)

            def turn_x(t):
                if isinstance(t, int):
                    pe.wait_ge(x_lo, 1 if t < 1 else 2 if t < 4 else 4)
                at_least(pe, xnT_sb, t - 1)
                for g in range(2):
                    mm = pe.transpose(t0[:, 3, g * P:(g + 1) * P],
                                      x_s[:, ds(2 * t + g, 1)].rearrange("p o k c -> p (o k c)"), ident[:])
                mm.then_inc(xT_ps, 1)

            def scores_of(u, g):
                pe.matmul(sc[g][:, 0:H * TP], ident[:], causal[:].rearrange("p h s -> p (h s)"), start=True, stop=False,
                          skip_group_check=True)
                for rows, heads, j, k_of in ((slice(0, P), slice(0, HA * TP), 0, k_a), (slice(0, R), slice(HA * TP, H * TP), 2, k_b)):
                    for a, b in ((0, 0), (1, 0), (0, 1)):
                        for c in range(NB):
                            q = slice(g * P + c * TP, g * P + (c + 1) * TP)
                            mm = pe.matmul(sc[g][c * TP:(c + 1) * TP, heads], qk_s[u][rows, j, a, q], k_of[u][:, b, :, q],
                                           start=False, stop=(j == 2 and b == 1), skip_group_check=True)
                mm.then_inc(sc_ps, 1)

            def step(t, u, i):
                if isinstance(t, int) and t == 1:
                    fold()
                if isinstance(t, int) and t == 0:
                    pe.wait_ge(consts, 3)
                    turn_x(0)
                if has(t, 1):
                    if isinstance(t, int) and t == 1:
                        pe.wait_ge(split_d, 2)
                    pe.wait_ge(xnT_sb, t)
                    at_least(pe, qk_lo, 2 * (t - 1))
                    for j in range(3):
                        dst = qk01[:, j * PW:(j + 1) * PW] if j < 2 else qk2[:, 0:PW]
                        for n, (k, w) in enumerate(parts(qkv_h, qkv_l)):
                            mm = pe.matmul(dst, w[:, j * P:(j + 1) * P], xnT[:, k, :], start=(n == 0), stop=(n == 4))
                        if j > 0:
                            mm.then_inc(qk_ps, 1)
                if has(t, 0):
                    if isinstance(t, int) and t == 0:
                        pe.wait_ge(split_d, 1)
                        pe.wait_ge(zeroed_x, 1)
                    pe.wait_ge(xT_sb, t + 1)
                    at_least(pe, v_lo, t - 1)
                    for g in range(2):
                        n = 0
                        for w in (tok_w_h, tok_w_l):
                            for half in range(2):
                                mm = pe.matmul(hv[:, g * D:(g + 1) * D], xT[:, g * P + half:g * P + half + P], w[:, half, :],
                                               start=(g == 0 and n == 0), stop=(n == 3), skip_group_check=True)
                                n += 1
                    mm.then_inc(tok_ps, 1)
                if has(t, -1):
                    turn_x(t + 1)
                if has(t, 5):
                    p = t - 5
                    pe.wait_ge(x2_hi, p + 1)
                    pe.wait_ge(x2_lo, p + 1)
                    for g in range(2):
                        mm = turn(t1, x2_s[:, g].rearrange("p k d -> p (k d)"), g * P)
                    mm.then_inc(x2T_ps, 1)
                if has(t, 2):
                    if isinstance(t, int) and t == 2:
                        pe.wait_ge(consts, 8)
                        pe.wait_ge(folded, 3)
                        pe.wait_ge(folded_d, 1)
                    pe.wait_ge(k_bd[u], 16 * (HA + HB) * i)
                    at_least(pe, sc_sb, t - 2)
                    scores_of(u, 0)
                if has(t, 4):
                    p = t - 4
                    pe.wait_ge(y_hi, p + 1)
                    pe.wait_ge(y_lo, p + 1)
                    at_least(pe, x2T_sb, p)
                    for g in range(2):
                        mm = turn(t1, y_s[:, g].rearrange("p k d -> p (k d)"), g * P)
                    mm.then_inc(yT_ps, 1)
                if has(t, 2):
                    scores_of(u, 1)
                if has(t, 4):
                    p = t - 4
                    if isinstance(t, int) and t == 4:
                        pe.wait_ge(split_d, 3)
                    pe.wait_ge(yT_sb, p + 1)
                    for g in range(2):
                        mm = rows_by_weights(yp[:, g * D:(g + 1) * D], yT, g * P, proj_h, proj_l, slice(0, D))
                    mm.then_inc(proj_ps, 1)
                if has(t, 1):
                    pe.wait_ge(h_sb, t + 1 if not isinstance(t, int) else min(t + 1, NPAIR))
                    for g in range(2):
                        mm = rows_by_weights(hv[:, g * D:(g + 1) * D], xnT, g * P, qkv_h, qkv_l, slice(2 * D, 3 * D))
                    mm.then_inc(v_ps, 1)
                if has(t, 0):
                    pe.wait_ge(xn_hi, t + 1)
                    pe.wait_ge(xn_lo, t + 1)
                    pe.wait_ge(xT_sb, t + 2 if not isinstance(t, int) else min(t + 2, NPAIR))
                    for g in range(2):
                        mm = turn(t0, xn_s[:, g].rearrange("p k d -> p (k d)"), g * P)
                    mm.then_inc(xnT_ps, 1)
                if has(t, 3):
                    p = t - 3
                    pe.wait_ge(pT_bd, 16 * NB * (p + 1))
                    at_least(pe, h2_sb, p)
                    pe.wait_ge(v_lo, p + 1)
                    for g in range(2):
                        for h_ in range(H):
                            o = (g * H + h_) * (HD + 1)
                            for n, (a, b) in enumerate(((0, 0), (1, 0), (0, 1))):
                                mm = pe.matmul(yp[:, o:o + HD + 1], p_bd[1 - u][:, g, a, :, h_], v_s[1 - u][:, g, b, h_, :],
                                               start=(g == 0 and h_ == 0 and n == 0), stop=(n == 2), skip_group_check=True)
                    mm.then_inc(pv_ps, 1)

            attention(pe, step)

            pe.wait_ge(split_d, 8)
            pe.wait_ge(consts, 11)
            pe.wait_ge(x2T_sb, NPAIR)
            pe.wait_ge(v_lo, NPAIR)
            for g in range(NG):
                for n, (k, w) in enumerate(parts(router_h, router_l)):
                    mm = pe.matmul(hv[:, g * E:(g + 1) * E], x2T[:, k, g * P:(g + 1) * P], w, start=(g == 0 and n == 0),
                                   stop=(n == 4), skip_group_check=True)
            mm.then_inc(logit_ps, 1)
            pe.wait_ge(router_d, 10 + E)

            def ffn_step(s, u, i):
                if not isinstance(s, int) or s < NBLK:
                    for g in range(4):
                        mm = pe.transpose(t0[:, g // 2, (g % 2) * P:(g % 2 + 1) * P],
                                          onehot[:, ds(4 * s + g, 1), :].rearrange("p o c -> p (o c)"), ident[:])
                    mm.then_inc(ohT_ps, 1)
                    for j in range(4):
                        at_least(pe, gh_sb, 4 * s + j - 3)
                        if j == 0:
                            pe.wait_ge(ohT_sb, s + 1)
                        pe.matmul(pre[j][:], lower[:, j, :], ohT[u][0:9, :], start=True, stop=False)
                        for n, (k, w) in enumerate(parts(w1_h, w1_l)):
                            mm = pe.matmul(pre[j][:], w[:, j * P:(j + 1) * P], x2T[:, k, ds(s * BW, BW)],
                                           start=False, stop=(n == 4))
                        mm.then_inc(pre_ps, 1)
                if not isinstance(s, int) or s >= 1:
                    q = s - 1
                    v = 1 - u
                    pe.wait_ge(gl_sb, 4 * q + 4)
                    at_least(pe, o_sb, q)
                    for g in range(4):
                        dst = ffn[g // 2][:, (g % 2) * D:(g % 2 + 1) * D]
                        c = slice(g * P, (g + 1) * P)
                        pe.matmul(dst, ohT[v][0:40, c], b2_parts[:], start=(g % 2 == 0), stop=False, skip_group_check=True)
                        for j in range(4):
                            pe.matmul(dst, g_h[v][:, j, c], w2_h[:, j, :], start=False, stop=False, skip_group_check=True)
                            pe.matmul(dst, g_l[v][:, j, c], w2_h[:, j, :], start=False, stop=False, skip_group_check=True)
                            mm = pe.matmul(dst, g_h[v][:, j, c], w2_l[:, j, :], start=False, stop=(j == 3), skip_group_check=True)
                        if g % 2:
                            mm.then_inc(ffn_ps, 1)

            pipeline(pe, ffn_step, NBLK, 1, 4, NBLK)


def kernel(x, L0_tok_W, L0_tok_b, L0_attn_W_attn, L0_attn_b_attn, L0_attn_W_proj, L0_attn_b_proj,
           L0_ffn_enc_w, L0_ffn_enc_b, L0_ffn_sw_w, L0_ffn_sw_b, L0_ffn_w1, L0_ffn_b1, L0_ffn_w2, L0_ffn_b2):
    import numpy as np
    import concourse.bacc as bacc
    from concourse.bass_utils import run_bass_kernel_spmd

    def stack(w):
        a = [w[0:64], w[64:128], w[128:192]]
        return np.stack([np.concatenate([a[0], a[1]]), np.concatenate([a[2], a[0]]), np.concatenate([a[1], a[2]])], axis=1)

    inputs = [np.asarray(v) for v in (x, L0_tok_W, L0_tok_b, L0_attn_W_attn, L0_attn_b_attn, L0_attn_W_proj, L0_attn_b_proj,
                                      L0_ffn_enc_w, L0_ffn_enc_b, L0_ffn_sw_w, L0_ffn_sw_b, L0_ffn_w1, L0_ffn_b1, L0_ffn_w2, L0_ffn_b2)]
    x, tok_W, tok_b, W_attn, b_attn, W_proj, b_proj, enc_w, enc_b, sw_w, sw_b, w1, b1, w2, b2 = inputs
    order = np.concatenate([np.arange(0, 128), np.arange(192, 320), np.arange(128, 192), np.arange(320, 384), np.arange(384, 576)])
    halves = [tok_W[:, 0:CH].T, tok_W[:, CH:].T]
    vb = b_attn[384:]
    first = np.zeros((P, FIRST), np.float32)
    first[:, 0:D] = tok_b
    first[:, D:D + 3] = b_attn[order[:384]].reshape(3, P).T
    first[:, D + 3:D + 7] = b1.reshape(4, P).T
    later = np.zeros((P, LATER), np.float32)
    later[:, 0:D] = b_proj
    later[:, D:D + E] = sw_b
    later[:, 200:328] = vb[0:128, None]
    later[0:R, 328:456] = vb[128:192, None]
    later[0:R, 456:584] = enc_b[:, None]
    later[0:R, 584:592] = sw_w
    later[0:R, 592:976] = np.concatenate([stack(enc_w)[:, n].T for n in range(3)], axis=1)
    later[0:E, 976:1168] = b2
    later[32:32 + E, 976:1168] = b2
    arrays = {
        "x": x,
        "tok_w": np.stack([np.concatenate([w, w]) for w in halves], axis=1),
        "first_rows": first,
        "qkv_w": stack(W_attn[:, order]),
        "proj_w": stack(W_proj),
        "later_rows": later,
        "w1": stack(w1.transpose(1, 0, 2).reshape(D, ER)),
        "w2": w2.reshape(4, P, D).transpose(1, 0, 2),
    }
    nc = bacc.Bacc("TRN2", target_bir_lowering=False, num_devices=1)
    feeds, args = {}, []
    for name, a in arrays.items():
        feeds[name + "_dram"] = np.ascontiguousarray(a)
        args.append(nc.dram_tensor(name + "_dram", a.shape, F32, kind="ExternalInput").ap())
    out = nc.dram_tensor("out_dram", (B, T, D), F32, kind="ExternalOutput").ap()
    audio_tower(nc, *args, out)
    result = run_bass_kernel_spmd(nc, [feeds], core_ids=[0])
    return result.results[0]["out_dram"]
```

```python
from contextlib import ExitStack

import concourse.bass as bass
from concourse import mybir

F32 = mybir.dt.float32
F16 = mybir.dt.float16
BF16 = mybir.dt.bfloat16
ALU = mybir.AluOpType
ACT = mybir.ActivationFunctionType
AX_X = mybir.AxisListType.X
ds = bass.ds

P = 128
B, T_IN, C_IN = 128, 256, 8
STRIDE = 8
CH = STRIDE * C_IN
T = T_IN // STRIDE - 1
TP = 32
D = 192
H, HD = 12, 16
HA, HB = 8, 4
NB = P // TP
NG = B // NB
NPAIR = NG // 2
NBLK = NG // 4
E, R = 8, 64
ER = E * R
WS = 64.0
EPS = 1e-5
MASKED = -1e30
OFF = 32768.0
PW = 2 * P
BW = 4 * P
FIRST = D + 7
LATER = 1168


def audio_tower(nc, x, tok_w, first_rows, qkv_w, proj_w, later_rows, w1, w2, out):
    x_rows = x.rearrange("b (c t) f -> (b c) (t f)", t=STRIDE).rearrange("(g p) f -> p g f", p=P)

    with ExitStack() as ctx:
        def sb(name, shape, dt=F32):
            return ctx.enter_context(nc.sbuf_tensor(name, shape, dt))

        def sem(name):
            return ctx.enter_context(nc.semaphore(name))

        tok_w_f = sb("tok_w_f", [P, 2, D])
        qkv_w_f = sb("qkv_w_f", [P, 3, 3 * D])
        proj_w_f = sb("proj_w_f", [P, 3, D])
        w1_f = sb("w1_f", [P, 3, ER])
        w2_f = sb("w2_f", [P, 4, D])
        first_f = sb("first_f", [P, FIRST])
        tok_b = first_f[:, 0:D]
        qk_b_f = first_f[:, D:D + 3]
        b1_f = first_f[:, D + 3:D + 7]
        later_f = sb("later_f", [P, LATER])
        proj_b = later_f[:, 0:D]
        sw_b = later_f[:, D:D + E]
        v_b_wide = later_f[:, 200:456].rearrange("p (k c) -> p k c", k=2)
        enc_b_wide = later_f[0:R, 456:584]
        sw_w_f = later_f[0:R, 584:592]
        enc_wt_f = later_f[0:R, 592:976].rearrange("p (k c) -> p k c", k=3)
        b2_f = later_f[96:96 + 2 * E, 976:1168]
        qk_b_s = sb("qk_b_s", [P, 3])
        tok_w_h = sb("tok_w_h", [P, 2, D], F16)
        tok_w_l = sb("tok_w_l", [P, 2, D], F16)
        qkv_h = sb("qkv_h", [P, 3, 3 * D], F16)
        qkv_l = sb("qkv_l", [P, 2, 3 * D], F16)
        proj_h = sb("proj_h", [P, 3, D], F16)
        proj_l = sb("proj_l", [P, 2, D], F16)
        w1_h = sb("w1_h", [P, 3, ER], F16)
        w1_l = sb("w1_l", [P, 2, ER], F16)
        w2_h = sb("w2_h", [P, 4, D], F16)
        w2_l = sb("w2_l", [P, 4, D], F16)
        router_f = sb("router_f", [P, 3, E])
        router_h = sb("router_h", [P, 3, E], F16)
        router_l = sb("router_l", [P, 2, E], F16)
        b2_mem = sb("b2_mem", [P, D], F16)
        b2_h = b2_mem[96:96 + 2 * E]
        b2_parts = sb("b2_parts", [P, D], F16)
        out_b = sb("out_b", [P, D])
        route_b = sb("route_b", [P, E])
        ident = sb("ident", [P, P], F16)
        causal = sb("causal", [P, H, TP], BF16)
        pick = sb("pick", [P, E])
        x_f = sb("x_f", [P, NG, CH])
        x_s = sb("x_s", [P, NG, 2, CH], F16)
        xT = sb("xT", [P, PW + 1], F16)
        h_all = sb("h_all", [P, NPAIR, 2, D])
        stats = sb("stats", [P, 2, 2, 6])
        mv = sb("mv", [P, 2, 2, 2])
        var_eps = sb("var_eps", [P, 2, 2])
        half = sb("half", [P, 2])
        rstd = sb("rstd", [P, 2, 2])
        xn_f = sb("xn_f", [P, 2, D])
        xn_s = sb("xn_s", [P, 2, 2, D], F16)
        xnT = sb("xnT", [P, 3, PW], F16)
        qk_s = [sb(f"qk_s{u}", [P, 3, 2, PW], F16) for u in range(2)]
        v_s = [sb(f"v_s{u}", [P, 2, 2, H, HD + 1], F16) for u in range(2)]
        k_a = [sb(f"k_a{u}", [P, 2, HA, PW], F16) for u in range(2)]
        k_b = [sb(f"k_b{u}", [HB * HD, 2, HB, PW], F16) for u in range(2)]
        top = sb("top", [P, 2, H])
        scores = sb("scores", [P, 2, H, TP])
        prob = sb("prob", [P, 2, H, TP])
        probT = sb("probT", [P, 2, TP, H])
        probT_s = sb("probT_s", [P, 2, 2, TP, H], F16)
        p_mem = [sb(f"p_mem{u}", [P, 4 * P * H], F16) for u in range(2)]
        p_bd = [m[:].rearrange("p (g k c h) -> p g k c h", g=2, k=2, h=H) for m in p_mem]
        rden = sb("rden", [P, 2, H])
        y_f = sb("y_f", [P, 2, H, HD])
        y_s = sb("y_s", [P, 2, 2, D], F16)
        yT = sb("yT", [P, 3, PW], F16)
        h = sb("h", [P, 2, D])
        spacer = sb("spacer", [P, 1])
        x2_f = sb("x2_f", [P, 2, D])
        x2_s = sb("x2_s", [P, 2, 2, D], F16)
        x2T = sb("x2T", [P, 3, NG * P], F16)
        logit = sb("logit", [P, NG, E])
        l_top = sb("l_top", [P, NG])
        l_exp = sb("l_exp", [P, NG, E])
        l_sum = sb("l_sum", [P, NG])
        p_top = sb("p_top", [P, NG])
        cand = sb("cand", [P, NG, E])
        c_top = sb("c_top", [P, NG])
        onehot = x_s[:].rearrange("p g k c -> p g (k c)")
        x2_oh = [sb(f"x2_oh{u}", [P, BW], F16) for u in range(2)]
        g_f = [x_f[:].rearrange("p g c -> p (g c)")[:, u * BW:(u + 1) * BW] for u in range(2)]
        g_h = [m[:, 0:4 * BW].rearrange("p (j c) -> p j c", j=4) for m in p_mem]
        g_l = [m[:, 4 * BW:8 * BW].rearrange("p (j c) -> p j c", j=4) for m in p_mem]
        o_f = [m[:, 8 * BW:8 * BW + 8 * D].bitcast(F32).rearrange("p (g d) -> p g d", g=4) for m in p_mem]

        bank = [ctx.enter_context(nc.psum_tensor(f"bank{i}", [P, 512], F32)) for i in range(8)]
        t0 = bank[0][:].bitcast(F16).rearrange("p (k c) -> p k c", k=4)
        t1 = bank[1][:].bitcast(F16).rearrange("p (k c) -> p k c", k=4)
        hv = bank[2]
        yp = bank[3]
        qk01, qk2 = bank[4], bank[5]
        sc = [bank[6], bank[7]]
        pre = [bank[2], bank[3], bank[4], bank[5]]
        ffn = [bank[6], bank[7]]

        w_load = {n: sem(f"{n}_load") for n in ("tok", "first", "qkv", "later", "ffn")}
        x_load = [sem(f"x_load{i}") for i in range(4)]
        consts = sem("consts")
        k_zeroed, p_zeroed, b2_zeroed = sem("k_zeroed"), sem("p_zeroed"), sem("b2_zeroed")
        zeroed_x = sem("zeroed_x")
        folded, folded_d = sem("folded"), sem("folded_d")
        split_a = sem("split_a")
        split_d = sem("split_d")
        x_hi = sem("x_hi")
        x_lo = sem("x_lo")
        xT_ps, xT_sb = sem("xT_ps"), sem("xT_sb")
        tok_ps, h_sb = sem("tok_ps"), sem("h_sb")
        bn1, ag1, rs1, xn_sb, xn_hi, xn_lo = (sem(n) for n in ("bn1", "ag1", "rs1", "xn_sb", "xn_hi", "xn_lo"))
        ve1, ve2 = sem("ve1"), sem("ve2")
        xnT_ps, xnT_sb = sem("xnT_ps"), sem("xnT_sb")
        qk_ps, qk_hi, qk_lo = sem("qk_ps"), sem("qk_hi"), sem("qk_lo")
        v_ps, v_hi, v_lo = sem("v_ps"), sem("v_hi"), sem("v_lo")
        k_bd = [sem(f"k_bd{u}") for u in range(2)]
        sc_ps, sc_top, sc_sb = sem("sc_ps"), sem("sc_top"), sem("sc_sb")
        pr_sb, pT_sb, pT_hi, pT_lo, pT_bd = (sem(n) for n in ("pr_sb", "pT_sb", "pT_hi", "pT_lo", "pT_bd"))
        pv_ps, rden_sb, y_sb, y_hi, y_lo = (sem(n) for n in ("pv_ps", "rden_sb", "y_sb", "y_hi", "y_lo"))
        yT_ps, yT_sb = sem("yT_ps"), sem("yT_sb")
        hb_sb, proj_ps, h2_sb = sem("hb_sb"), sem("proj_ps"), sem("h2_sb")
        bn2, ag2, rs2, x2_sb, x2_hi, x2_lo = (sem(n) for n in ("bn2", "ag2", "rs2", "x2_sb", "x2_hi", "x2_lo"))
        x2T_ps, x2T_sb = sem("x2T_ps"), sem("x2T_sb")
        logit_ps, logit_sb, oh_zeroed, pick_set = (sem(n) for n in ("logit_ps", "logit_sb", "oh_zeroed", "pick_set"))
        router_d, router_a = sem("router_d"), sem("router_a")
        ohT_ps, ohT_sb, x2c_sb = sem("ohT_ps"), sem("ohT_sb"), sem("x2c_sb")
        pre_ps, g_sb, gh_sb, gl_sb = sem("pre_ps"), sem("g_sb"), sem("gh_sb"), sem("gl_sb")
        ffn_ps, o_sb, stored = sem("ffn_ps"), sem("o_sb"), sem("stored")

        X_CUTS = [0, 2, 8, 16, NG]

        def at_least(eng, s, n):
            if not isinstance(n, int) or n > 0:
                eng.wait_ge(s, n)

        def pipeline(eng, step, n, ahead, first, last):
            for t in range(first):
                step(t, t % 2, t // 2)
            with eng.Fori(first // 2, last // 2) as i:
                for u in range(2):
                    step(2 * i + u, u, i)
            for t in range(last, n + ahead):
                step(t, t % 2, t // 2)

        STAGES = 6

        def attention(eng, step, steps=NPAIR + STAGES - 1):
            pipeline(eng, step, NPAIR, steps - NPAIR, STAGES, NPAIR - 2)

        DRAIN = NPAIR + 1
        HALF = NG // 2
        ALONE = 3

        def pre_bank(s, j):
            return pre[2 + j % 2] if isinstance(s, int) and s < ALONE else pre[j]

        def has(t, lag):
            return not isinstance(t, int) or 0 <= t - lag < NPAIR

        block = ctx.enter_context(nc.Block())

        @block.sync
        def _(sp):
            sp.dma_start(x_f[:, 0:2, :], x_rows[:, 0:2, :]).then_inc(x_load[0], 16)
            sp.dma_start(tok_w_f[:], tok_w).then_inc(w_load["tok"], 16)
            sp.dma_start(first_f[:], first_rows).then_inc(w_load["first"], 16)
            sp.dma_start(qkv_w_f[:], qkv_w).then_inc(w_load["qkv"], 16)
            sp.dma_start(x_f[:, 2:8, :], x_rows[:, 2:8, :]).then_inc(x_load[1], 16)
            sp.dma_start(proj_w_f[:], proj_w).then_inc(w_load["later"], 16)
            sp.dma_start(later_f[:], later_rows).then_inc(w_load["later"], 16)
            for i in range(2, 4):
                a, b = X_CUTS[i], X_CUTS[i + 1]
                sp.dma_start(x_f[:, a:b, :], x_rows[:, a:b, :]).then_inc(x_load[i], 16)
            sp.dma_start(w1_f[:], w1).then_inc(w_load["ffn"], 16)
            sp.dma_start(w2_f[:], w2).then_inc(w_load["ffn"], 16)

            def step(t, u, i):
                if has(t, 1):
                    if isinstance(t, int) and t < 3:
                        sp.wait_ge(k_zeroed, t)
                    sp.wait_ge(qk_hi, 2 * t)
                    sp.wait_ge(qk_lo, 2 * t)
                    for h in range(HA):
                        r = slice(h * HD, (h + 1) * HD)
                        sp.dma_start(k_a[1 - u][r, :, h, :], qk_s[1 - u][r, 1, :, :]).then_inc(k_bd[1 - u], 16)
                    for h in range(HB):
                        r = slice(h * HD, (h + 1) * HD)
                        s = slice(R + h * HD, R + (h + 1) * HD)
                        sp.dma_start(k_b[1 - u][r, :, h, :], qk_s[1 - u][s, 2, :, :]).then_inc(k_bd[1 - u], 16)
                if has(t, 2):
                    if isinstance(t, int) and t < 4:
                        sp.wait_ge(p_zeroed, t - 1)
                    sp.wait_ge(pT_hi, t - 1)
                    sp.wait_ge(pT_lo, t - 1)
                    for b in range(NB):
                        r = slice(b * TP, (b + 1) * TP)
                        sp.dma_start(p_bd[u][r, :, :, r, :], probT_s[r]).then_inc(pT_bd, 16)

            attention(sp, step)

            for s in range(NBLK):
                sp.wait_ge(o_sb, s + 1)
                at_least(sp, stored, 16 * NB * s)
                for b in range(NB):
                    dst = out.rearrange("(s g b) t d -> s b t g d", g=4, b=NB)[s, b]
                    sp.dma_start(dst, o_f[s % 2][b * TP:b * TP + T, :, :]).then_inc(stored, 16)
            sp.wait_ge(stored, 16 * NB * NBLK)

        @block.gpsimd
        def _(pool):
            made = [0]

            def make(ins):
                ins.then_inc(consts, 1)
                made[0] += 1
                pool.wait_ge(consts, made[0])

            make(pool.memset(half[:], -0.5))
            make(pool.memset(ident[:], 0.0))
            make(pool.affine_select(out=ident[:], in_=ident[:], compare_op=ALU.not_equal, fill=1.0, base=0,
                                    pattern=[[-1, P]], channel_multiplier=1))
            make(pool.memset(causal[:], 0.0))
            for b in range(NB):
                r = slice(b * TP, (b + 1) * TP)
                make(pool.affine_select(out=causal[r], in_=causal[r], compare_op=ALU.is_ge, fill=MASKED, base=0,
                                        pattern=[[0, H], [-1, TP]], channel_multiplier=1))

            def zero_k(u):
                pool.memset(k_b[u][:].bitcast(F32), 0.0)
                pool.memset(k_a[u][:].bitcast(F32), 0.0).then_inc(k_zeroed, 1)

            def zero_p(u):
                pool.memset(p_mem[u][:].bitcast(F32), 0.0).then_inc(p_zeroed, 1)

            def make_marks():
                make(pool.memset(w1_l[:, 1, :], 0.0))
                marks = w1_l[R:R + E, 1, :].rearrange("e (k r) -> e k r", k=E)
                make(pool.affine_select(out=marks, in_=marks, compare_op=ALU.not_equal, fill=-OFF, base=0,
                                        pattern=[[-1, E], [0, R]], channel_multiplier=1))
                pool.wait_ge(split_a, 5)
                make(pool.affine_select(out=b2_h, in_=b2_h, compare_op=ALU.is_ge, fill=0.0, base=-E,
                                        pattern=[[0, D]], channel_multiplier=1))

            def rstd_x2(p):
                pool.wait_ge(ve2, p + 1)
                pool.tensor_tensor(rstd[:, 1, :], var_eps[:, 1, :], half[:], ALU.pow).then_inc(rs2, 1)

            def prob_low(p):
                pool.wait_ge(pT_hi, p + 1)
                pool.tensor_tensor(probT_s[:, :, 1], probT[:], probT_s[:, :, 0], ALU.subtract).then_inc(pT_lo, 1)

            def x2_low(p):
                pool.wait_ge(x2_hi, p + 1)
                pool.tensor_tensor(x2_s[:, :, 1, :], x2_f[:], x2_s[:, :, 0, :], ALU.subtract).then_inc(x2_lo, 1)

            def y_low(p):
                pool.wait_ge(y_hi, p + 1)
                pool.tensor_tensor(y_s[:, :, 1, :], y_f[:].rearrange("p g h d -> p g (h d)"), y_s[:, :, 0, :],
                                   ALU.subtract).then_inc(y_lo, 1)

            def step(t, u, i):
                if has(t, 0):
                    pool.wait_ge(ve1, t + 1)
                    pool.tensor_tensor(rstd[:, 0, :], var_eps[:, 0, :], half[:], ALU.pow).then_inc(rs1, 1)
                    pool.wait_ge(xn_hi, t + 1)
                    pool.tensor_tensor(xn_s[:, :, 1, :], xn_f[:], xn_s[:, :, 0, :], ALU.subtract).then_inc(xn_lo, 1)
                    if isinstance(t, int) and t == 0:
                        zero_k(0)
                        zero_k(1)
                    if isinstance(t, int) and t in (1, 2):
                        zero_p(t - 1)
                    if isinstance(t, int) and t == 3:
                        make_marks()
                    if isinstance(t, int) and t == 0:
                        pool.wait_ge(folded, 3)
                    pool.tensor_tensor(h_all[:, t], h[:], out_b[:].unsqueeze(1).to_broadcast([P, 2, D]),
                                       ALU.add).then_inc(hb_sb, 1)
                if has(t, 4):
                    rstd_x2(t - 4)
                if has(t, 2):
                    prob_low(t - 2)
                if has(t, 4):
                    x2_low(t - 4)
                if has(t, 3):
                    y_low(t - 3)
                if isinstance(t, int) and t == NPAIR - 2:
                    pool.wait_ge(xT_ps, NPAIR)
                    pool.memset(x_s[:].bitcast(F32), 0.0).then_inc(oh_zeroed, 1)

            attention(pool, step, DRAIN)

            prob_low(NPAIR - 1)
            rstd_x2(NPAIR - 3)
            x2_low(NPAIR - 3)
            y_low(NPAIR - 2)
            rstd_x2(NPAIR - 2)
            x2_low(NPAIR - 2)
            y_low(NPAIR - 1)
            rstd_x2(NPAIR - 1)
            x2_low(NPAIR - 1)

        @block.scalar
        def _(act):
            def hi(dst, src):
                return act.activation(dst, src, ACT.Copy, scale=WS)

            def x_part(i):
                a, b = X_CUTS[i], X_CUTS[i + 1]
                act.wait_ge(x_load[i], 16)
                act.copy(x_s[:, a:b, 0, :], x_f[:, a:b, :]).then_inc(x_hi, 1)

            def x_turned(t):
                act.wait_ge(xT_ps, t + 1)
                at_least(act, tok_ps, t)
                act.copy(xT[:, 0:PW].rearrange("p (g c) -> p g c", g=2),
                         t0[:, 3:4, :].rearrange("p o (g c) -> p (o g) c", g=2)).then_inc(xT_sb, 1)

            def setup(t):
                if t == 0:
                    x_part(0)
                    act.wait_ge(w_load["tok"], 16)
                    hi(tok_w_h[:], tok_w_f[:]).then_inc(split_a, 1)
                    x_turned(0)
                    x_part(1)
                    act.wait_ge(w_load["first"], 16)
                    hi(qk_b_s[:], qk_b_f).then_inc(split_a, 1)
                    act.wait_ge(w_load["qkv"], 16)
                    hi(qkv_h[:], qkv_w_f[:]).then_inc(split_a, 1)
                if t == 1:
                    act.wait_ge(w_load["later"], 32)
                    hi(proj_h[:], proj_w_f[:]).then_inc(split_a, 1)
                    x_part(2)
                    x_part(3)
                if t == 2:
                    hi(b2_h, b2_f).then_inc(split_a, 1)
                    act.wait_ge(w_load["ffn"], 32)
                    hi(w1_h[:], w1_f[:]).then_inc(split_a, 1)
                if t == 3:
                    hi(w2_h[:], w2_f[:]).then_inc(split_a, 1)
                    act.wait_ge(folded, 3)
                    hi(router_h[:], router_f[:]).then_inc(split_a, 1)
                if t == NPAIR:
                    route_exp(0, HALF, 0)

            def x2_turned(p):
                act.wait_ge(x2T_ps, p + 1)
                act.copy(x2T[:, :, ds(p * PW, PW)], t1[:, 0:3, :]).then_inc(x2T_sb, 1)

            def y_turned(p):
                act.wait_ge(yT_ps, p + 1)
                at_least(act, proj_ps, p)
                act.copy(yT[:], t1[:, 0:3, :]).then_inc(yT_sb, 1)

            def x2_high(p):
                act.wait_ge(x2_sb, p + 1)
                at_least(act, x2T_ps, p)
                act.copy(x2_s[:, :, 0, :], x2_f[:]).then_inc(x2_hi, 1)

            def y_high(p):
                act.wait_ge(y_sb, p + 1)
                at_least(act, yT_ps, p)
                act.copy(y_s[:, :, 0, :], y_f[:].rearrange("p g h d -> p g (h d)")).then_inc(y_hi, 1)

            def route_exp(a, b, n):
                act.wait_ge(router_d, n + 2)
                act.activation(l_exp[:, a:b], l_exp[:, a:b], ACT.Exp).then_inc(router_a, 1)

            def marks(s, u):
                act.wait_ge(ohT_ps, s + 1)
                act.copy(x2_oh[u][R:P], t0[R:P, 0:2, :].rearrange("p k c -> p (k c)")).then_inc(ohT_sb, 1)

            def gelu_full(s, j):
                act.wait_ge(pre_ps, 4 * s + j + 1)
                at_least(act, gl_sb, 4 * s + j - 1)
                act.activation(g_f[j % 2], pre_bank(s, j)[:], ACT.Gelu, bias=b1_f[:, j:j + 1], scale=1.0 / WS).then_inc(g_sb, 1)

            def gelu_high(s, u, j):
                act.activation(g_h[u][:, j, :], pre_bank(s, j)[:], ACT.Gelu, bias=b1_f[:, j:j + 1],
                               scale=1.0 / WS).then_inc(gh_sb, 1)

            def gelu(s, u, j):
                gelu_full(s, j)
                gelu_high(s, u, j)

            def exp_scores(p):
                act.wait_ge(sc_sb, p + 1)
                at_least(act, pT_sb, p)
                act.activation(prob[:], scores[:], ACT.Exp, scale=0.25 / (WS * WS)).then_inc(pr_sb, 1)

            def prob_high(p):
                act.wait_ge(pT_sb, p + 1)
                at_least(act, pT_bd, 16 * NB * p)
                act.copy(probT_s[:, :, 0], probT[:]).then_inc(pT_hi, 1)

            def step(t, u, i):
                if isinstance(t, int):
                    setup(t)
                if has(t, 1):
                    w = 1 - u
                    act.wait_ge(qk_ps, 2 * t - 1)
                    for j in range(2):
                        mm = act.activation(qk_s[w][:, j, 0, :], qk01[:, j * PW:(j + 1) * PW], ACT.Identity,
                                            bias=qk_b_s[:, j:j + 1])
                    mm.then_inc(qk_hi, 1)
                    act.wait_ge(qk_ps, 2 * t)
                    act.activation(qk_s[w][:, 2, 0, :], qk2[:, 0:PW], ACT.Identity, bias=qk_b_s[:, 2:3]).then_inc(qk_hi, 1)
                if has(t, -1):
                    x_turned(t + 1)
                if has(t, 5):
                    x2_turned(t - 5)
                if has(t, 4):
                    y_turned(t - 4)
                if has(t, 0):
                    act.wait_ge(xn_sb, t + 1)
                    at_least(act, xnT_ps, t)
                    act.copy(xn_s[:, :, 0, :], xn_f[:]).then_inc(xn_hi, 1)
                if has(t, 2):
                    exp_scores(t - 2)
                if isinstance(t, int) and t == NPAIR:
                    marks(0, 0)
                if has(t, 0):
                    act.wait_ge(xnT_ps, t + 1)
                    at_least(act, v_ps, t)
                    act.copy(xnT[:], t0[:, 0:3, :]).then_inc(xnT_sb, 1)
                if has(t, 2):
                    prob_high(t - 2)
                if has(t, 1):
                    act.wait_ge(v_ps, t)
                    at_least(act, pv_ps, t - 2)
                    act.copy(v_s[1 - u][:, :, 0, :, 0:HD],
                             hv[:, 0:2 * D].rearrange("p (g h d) -> p g h d", g=2, h=H)).then_inc(v_hi, 1)
                if has(t, 3):
                    y_high(t - 3)
                if has(t, 4):
                    x2_high(t - 4)

            attention(act, step, DRAIN)

            def ffn_step(s, u, i):
                marks(s, u)
                for j in range(4):
                    gelu(s, u, j)

            x2_turned(NPAIR - 4)
            exp_scores(NPAIR - 1)
            y_turned(NPAIR - 3)
            prob_high(NPAIR - 1)
            gelu_full(0, 0)
            act.wait_ge(pv_ps, NPAIR - 1)
            gelu_high(0, 0, 0)
            x2_high(NPAIR - 3)
            y_high(NPAIR - 2)
            gelu(0, 0, 1)
            gelu(0, 0, 2)
            x2_turned(NPAIR - 3)
            gelu(0, 0, 3)
            y_turned(NPAIR - 2)
            x2_high(NPAIR - 2)
            marks(1, 1)
            y_high(NPAIR - 1)
            gelu(1, 1, 0)
            x2_turned(NPAIR - 2)
            gelu(1, 1, 1)
            y_turned(NPAIR - 1)
            gelu(1, 1, 2)
            gelu(1, 1, 3)
            marks(2, 0)
            x2_high(NPAIR - 1)
            gelu(2, 0, 0)
            gelu(2, 0, 1)
            x2_turned(NPAIR - 1)
            gelu(2, 0, 2)
            gelu(2, 0, 3)
            marks(3, 1)
            route_exp(HALF, NG, 12)
            for j in range(4):
                gelu(3, 1, j)
            with act.Fori(2, NBLK // 2) as i:
                for u in range(2):
                    ffn_step(2 * i + u, u, i)

        @block.vector
        def _(dve):
            def lo(dst, src, high):
                return dve.scalar_tensor_tensor(out=dst, in0=src, scalar=WS, in1=high, op0=ALU.mult, op1=ALU.subtract)

            def x_part(i):
                a, b = X_CUTS[i], X_CUTS[i + 1]
                dve.wait_ge(x_hi, i + 1)
                dve.tensor_tensor(x_s[:, a:b, 1, :], x_f[:, a:b, :], x_s[:, a:b, 0, :], ALU.subtract).then_inc(x_lo, 1)

            def setup(t):
                if t == 0:
                    dve.memset(xT[:, PW:PW + 1], 0.0).then_inc(zeroed_x, 1)
                    x_part(0)
                    dve.wait_ge(split_a, 1)
                    lo(tok_w_l[:], tok_w_f[:], tok_w_h[:]).then_inc(split_d, 1)
                    for u in range(2):
                        dve.memset(v_s[u][:, :, 0, :, HD:HD + 1], WS)
                        dve.memset(v_s[u][:, :, 1, :, HD:HD + 1], 0.0)
                    dve.memset(b2_parts[:], 0.0).then_inc(b2_zeroed, 1)
                    for e in range(E):
                        mm = dve.memset(pick[:, e:e + 1], float(E - e))
                    mm.then_inc(pick_set, 1)
                if t == 1:
                    dve.wait_ge(split_a, 3)
                    lo(qkv_l[:], qkv_w_f[:, 0:2, :], qkv_h[:, 0:2, :]).then_inc(split_d, 1)
                    dve.wait_ge(folded, 1)
                    dve.tensor_copy(router_f[:], sc[0][:, 0:3 * E].rearrange("p (k e) -> p k e", k=3)).then_inc(folded_d, 1)
                    dve.tensor_tensor(out_b[:], sc[1][:, 0:D], proj_b, ALU.add).then_inc(folded, 1)
                    dve.tensor_tensor(route_b[:], sc[1][:, D:D + E], sw_b, ALU.add).then_inc(folded, 1)
                if t == 2:
                    x_part(2)
                    x_part(3)
                    dve.wait_ge(split_a, 4)
                    lo(proj_l[:], proj_w_f[:, 0:2, :], proj_h[:, 0:2, :]).then_inc(split_d, 1)
                if t == 4:
                    dve.wait_ge(split_a, 8)
                    lo(router_l[:], router_f[:, 0:2, :], router_h[:, 0:2, :]).then_inc(split_d, 1)
                    dve.wait_ge(b2_zeroed, 1)
                    dve.wait_ge(consts, 11)
                    lo(b2_parts[96:96 + 2 * E], b2_f, b2_h).then_inc(split_d, 1)
                    lo(w1_l[:, 0, :], w1_f[:, 0, :], w1_h[:, 0, :])
                    lo(w1_l[0:R, 1, :], w1_f[0:R, 1, :], w1_h[0:R, 1, :]).then_inc(split_d, 1)
                if t == 5:
                    lo(w2_l[:], w2_f[:], w2_h[:]).then_inc(split_d, 1)
                if t == NPAIR - 1:
                    dve.wait_ge(pick_set, 1)
                    route_top(0, HALF, 0)
                if t == NPAIR:
                    dve.wait_ge(oh_zeroed, 1)
                    route_marks(0, HALF, 0)

            def row_stats(k, rows, bn):
                for g in range(2):
                    dve.bn_stats(stats[:, k, g, :], rows[:, g, :]).then_inc(bn, 1)

            def row_means(p, k, bn, ag):
                dve.wait_ge(bn, 2 * p + 2)
                dve.memset(spacer[:], 0.0)
                for g in range(2):
                    dve.bn_aggr(mv[:, k, g, :], stats[:, k, g, :]).then_inc(ag, 1)

            def row_var(p, k, ag, ve):
                dve.wait_ge(ag, 2 * p + 2)
                dve.tensor_scalar(var_eps[:, k, :], mv[:, k, :, 1], EPS, None, ALU.add).then_inc(ve, 1)

            def centre(p, k, rows, dst, rs, done):
                dve.wait_ge(rs, p + 1)
                for g in range(2):
                    mm = dve.tensor_scalar(dst[:, g, :], rows[:, g, :], mv[:, k, g, 0:1], rstd[:, k, g:g + 1],
                                           ALU.subtract, ALU.mult)
                mm.then_inc(done, 1)

            def scores_top(p, g):
                s = sc[g][:, 0:H * TP].rearrange("p (h s) -> p h s", h=H)
                dve.wait_ge(sc_ps, 2 * p + g + 1)
                dve.tensor_reduce(top[:, g, :], s, AX_X, ALU.max).then_inc(sc_top, 1)

            def scores_less_top(p, g):
                s = sc[g][:, 0:H * TP].rearrange("p (h s) -> p h s", h=H)
                dve.wait_ge(sc_top, 2 * p + g + 1)
                if g == 0:
                    at_least(dve, pr_sb, p)
                mm = dve.tensor_tensor(scores[:, g], s, top[:, g, :].unsqueeze(2).to_broadcast([P, H, TP]),
                                       ALU.subtract)
                if g == 1:
                    mm.then_inc(sc_sb, 1)

            def residual(p):
                dve.wait_ge(proj_ps, p + 1)
                dve.wait_ge(hb_sb, p + 1)
                dve.scalar_tensor_tensor(out=h_all[:, p], in0=yp[:, 0:2 * D].rearrange("p (g d) -> p g d", g=2),
                                         scalar=1.0 / WS, in1=h_all[:, p], op0=ALU.mult, op1=ALU.add).then_inc(h2_sb, 1)
                dve.wait_ge(h2_sb, p + 1)
                dve.memset(spacer[:], 0.0)
                row_stats(1, h_all[:, p], bn2)

            def residual_spread(p):
                row_means(p, 1, bn2, ag2)
                row_var(p, 1, ag2, ve2)

            def centre_x2(p):
                at_least(dve, x2_hi, p)
                at_least(dve, x2_lo, p)
                centre(p, 1, h_all[:, p], x2_f, rs2, x2_sb)

            def divide(p):
                dve.wait_ge(pv_ps, p + 1)
                yv = yp[:, 0:2 * H * (HD + 1)].rearrange("p (g h d) -> p g h d", g=2, h=H)
                dve.reciprocal(rden[:], yv[:, :, :, HD]).then_inc(rden_sb, 1)
                dve.wait_ge(rden_sb, p + 1)
                at_least(dve, y_hi, p)
                at_least(dve, y_lo, p)
                dve.tensor_tensor(y_f[:], yv[:, :, :, 0:HD], rden[:].unsqueeze(3).to_broadcast([P, 2, H, HD]),
                                  ALU.mult).then_inc(y_sb, 1)

            def logits_in(p):
                dve.wait_ge(logit_ps, p + 1)
                dve.scalar_tensor_tensor(out=logit[:, ds(2 * p, 2), :],
                                         in0=hv[:, 2 * D:2 * D + 2 * E].rearrange("p (g e) -> p g e", g=2), scalar=1.0 / WS,
                                         in1=route_b[:].unsqueeze(1).to_broadcast([P, 2, E]),
                                         op0=ALU.mult, op1=ALU.add).then_inc(logit_sb, 1)

            def wide(v, a, b):
                return v[:, a:b].unsqueeze(2).to_broadcast([P, b - a, E])

            def route_top(a, b, n):
                dve.wait_ge(logit_sb, b // 2)
                dve.tensor_reduce(l_top[:, a:b], logit[:, a:b], AX_X, ALU.max).then_inc(router_d, 1)
                dve.wait_ge(router_d, n + 1)
                dve.tensor_tensor(l_exp[:, a:b], logit[:, a:b], wide(l_top, a, b), ALU.subtract).then_inc(router_d, 1)
                dve.tensor_tensor(cand[:, a:b], logit[:, a:b], wide(l_top, a, b), ALU.is_equal).then_inc(router_d, 1)
                dve.wait_ge(router_d, n + 3)
                dve.tensor_tensor(cand[:, a:b], cand[:, a:b], pick[:].unsqueeze(1).to_broadcast([P, b - a, E]),
                                  ALU.mult).then_inc(router_d, 1)

            def route_marks(a, b, n):
                dve.wait_ge(router_d, n + 4)
                dve.tensor_reduce(c_top[:, a:b], cand[:, a:b], AX_X, ALU.max).then_inc(router_d, 1)
                dve.wait_ge(router_d, n + 5)
                dve.tensor_tensor(onehot[:, a:b, R:R + E], cand[:, a:b], wide(c_top, a, b), ALU.not_equal).then_inc(router_d, 1)
                for c in (96, 96 + E):
                    dve.tensor_tensor(onehot[:, a:b, c:c + E], cand[:, a:b], wide(c_top, a, b), ALU.is_equal).then_inc(router_d, 1)
                dve.wait_ge(router_d, n + 6)
                dve.tensor_scalar(onehot[:, a:b, R:R + E], onehot[:, a:b, R:R + E], 64.0, None, ALU.mult).then_inc(router_d, 1)

            def route_prob(a, b, n):
                dve.wait_ge(router_a, b // HALF)
                dve.tensor_reduce(l_sum[:, a:b], l_exp[:, a:b], AX_X, ALU.add).then_inc(router_d, 1)
                dve.wait_ge(router_d, n + 10)
                dve.reciprocal(l_top[:, a:b], l_sum[:, a:b]).then_inc(router_d, 1)
                dve.wait_ge(router_d, n + 11)
                dve.tensor_scalar(p_top[:, a:b], l_top[:, a:b], 1.0 / WS, None, ALU.mult).then_inc(router_d, 1)
                dve.wait_ge(router_d, n + 12)

            def features(s, u):
                dve.wait_ge(ohT_ps, s + 1)
                dve.tensor_copy(x2_oh[u][0:R], x2T[0:R, 1, ds(s * BW, BW)]).then_inc(x2c_sb, 1)

            def turn_prob(p):
                dve.wait_ge(pr_sb, p + 1)
                at_least(dve, pT_hi, p)
                at_least(dve, pT_lo, p)
                dve.transpose(probT[:].rearrange("p g t h -> p g h t"), prob[:]).then_inc(pT_sb, 1)

            def low_qk(t, w, j):
                if j != 1:
                    dve.wait_ge(qk_hi, 2 * t - 1 + j // 2)
                src = qk01[:, j * PW:(j + 1) * PW] if j < 2 else qk2[:, 0:PW]
                mm = dve.scalar_tensor_tensor(out=qk_s[w][:, j, 1, :], in0=src, scalar=qk_b_s[:, j:j + 1],
                                              in1=qk_s[w][:, j, 0, :], op0=ALU.add, op1=ALU.subtract)
                if j > 0:
                    mm.then_inc(qk_lo, 1)

            def step(t, u, i):
                if isinstance(t, int):
                    setup(t)
                if has(t, 0):
                    dve.wait_ge(tok_ps, t + 1)
                    if isinstance(t, int) and t == 0:
                        dve.wait_ge(w_load["first"], 16)
                    at_least(dve, hb_sb, t)
                    dve.scalar_tensor_tensor(out=h[:], in0=hv[:, 0:2 * D].rearrange("p (g d) -> p g d", g=2),
                                             scalar=1.0 / WS, in1=tok_b.unsqueeze(1).to_broadcast([P, 2, D]),
                                             op0=ALU.mult, op1=ALU.add).then_inc(h_sb, 1)
                    dve.wait_ge(h_sb, t + 1)
                    row_stats(0, h, bn1)
                if has(t, 1):
                    low_qk(t, 1 - u, 0)
                if has(t, 0):
                    row_means(t, 0, bn1, ag1)
                if has(t, 1):
                    low_qk(t, 1 - u, 1)
                if has(t, 0):
                    row_var(t, 0, ag1, ve1)
                    if isinstance(t, int) and t == 0:
                        x_part(1)
                if has(t, 1):
                    low_qk(t, 1 - u, 2)
                if has(t, 2):
                    scores_top(t - 2, 0)
                if has(t, 0):
                    at_least(dve, xn_hi, t)
                    at_least(dve, xn_lo, t)
                    centre(t, 0, h, xn_f, rs1, xn_sb)
                if has(t, 2):
                    scores_top(t - 2, 1)
                    scores_less_top(t - 2, 0)
                    scores_less_top(t - 2, 1)
                if has(t, 4):
                    residual(t - 4)
                if isinstance(t, int) and t == NPAIR:
                    features(0, 0)
                if has(t, 2):
                    turn_prob(t - 2)
                if has(t, 4):
                    residual_spread(t - 4)
                if has(t, 3):
                    divide(t - 3)
                if has(t, 1):
                    dve.wait_ge(v_hi, t)
                if has(t, 5):
                    logits_in(t - 5)
                if has(t, 1):
                    w = 1 - u
                    dve.tensor_tensor(v_s[w][:, :, 1, :, 0:HD], hv[:, 0:2 * D].rearrange("p (g h d) -> p g h d", g=2, h=H),
                                      v_s[w][:, :, 0, :, 0:HD], ALU.subtract).then_inc(v_lo, 1)
                if has(t, 4):
                    centre_x2(t - 4)

            attention(dve, step, DRAIN)

            def gelu_low(s, u, j):
                dve.wait_ge(gh_sb, 4 * s + j + 1)
                dve.tensor_tensor(g_l[u][:, j, :], g_f[j % 2], g_h[u][:, j, :], ALU.subtract).then_inc(gl_sb, 1)

            def result(q, u, k):
                dve.wait_ge(ffn_ps, 2 * q + k + 1)
                if k == 0:
                    at_least(dve, stored, 16 * NB * q)
                for g in (2 * k, 2 * k + 1):
                    mm = dve.scalar_tensor_tensor(out=o_f[u][:, g, :], in0=ffn[k][:, (g % 2) * D:(g % 2 + 1) * D],
                                                  scalar=p_top[:, ds(4 * q + g, 1)],
                                                  in1=h_all[:, ds(2 * q + k, 1), g % 2, :].rearrange("p o d -> p (o d)"),
                                                  op0=ALU.mult, op1=ALU.add)
                if k == 1:
                    mm.then_inc(o_sb, 1)

            def ffn_step(s, u, i):
                if not isinstance(s, int) or s < NBLK:
                    features(s, u)
                    for j in range(4):
                        gelu_low(s, u, j)
                for k in range(2):
                    result(s - 1, 1 - u, k)

            for g in range(2):
                scores_top(NPAIR - 1, g)
                scores_less_top(NPAIR - 1, g)
            turn_prob(NPAIR - 1)
            residual(NPAIR - 3)
            residual_spread(NPAIR - 3)
            divide(NPAIR - 2)
            logits_in(NPAIR - 4)
            centre_x2(NPAIR - 3)
            gelu_low(0, 0, 0)
            route_prob(0, HALF, 0)
            for j in range(1, 4):
                gelu_low(0, 0, j)
            result(0, 0, 0)
            residual(NPAIR - 2)
            residual_spread(NPAIR - 2)
            logits_in(NPAIR - 3)
            features(1, 1)
            centre_x2(NPAIR - 2)
            divide(NPAIR - 1)
            result(0, 0, 1)
            for j in range(3):
                gelu_low(1, 1, j)
            residual(NPAIR - 1)
            residual_spread(NPAIR - 1)
            logits_in(NPAIR - 2)
            gelu_low(1, 1, 3)
            centre_x2(NPAIR - 1)
            features(2, 0)
            gelu_low(2, 0, 0)
            result(1, 1, 0)
            result(1, 1, 1)
            logits_in(NPAIR - 1)
            route_top(HALF, NG, 12)
            gelu_low(2, 0, 1)
            route_marks(HALF, NG, 12)
            gelu_low(2, 0, 2)
            gelu_low(2, 0, 3)
            ffn_step(3, 1, 1)
            route_prob(HALF, NG, 12)
            with dve.Fori(2, NBLK // 2) as i:
                for u in range(2):
                    ffn_step(2 * i + u, u, i)
            ffn_step(NBLK, 0, NBLK // 2)

        @block.tensor
        def _(pe):
            def parts(w_h, w_l):
                return [(0, w_h[:, 0]), (1, w_h[:, 1]), (2, w_h[:, 2]), (0, w_l[:, 0]), (1, w_l[:, 1])]

            def rows_by_weights(dst, actT, c0, w_h, w_l, cols):
                five = parts(w_h, w_l)
                for n, (k, w) in enumerate(five):
                    mm = pe.matmul(dst, actT[:, k, c0:c0 + P], w[:, cols], start=(n == 0), stop=(n == 4))
                return mm

            def turn(bank_t, src, c0):
                for k in range(3):
                    mm = pe.transpose(bank_t[:, k, c0:c0 + P], src[:, k * P:(k + 1) * P], ident[:])
                return mm

            def fold():
                pe.wait_ge(w_load["later"], 32)
                for k in range(3):
                    pe.matmul(sc[0][:, k * E:(k + 1) * E], enc_wt_f[:, k, :], sw_w_f, start=(k == 0), stop=True,
                              skip_group_check=True)
                pe.matmul(sc[1][:, 0:D], v_b_wide[:, 0, :], proj_w_f[:, 0, :], start=True, stop=False, skip_group_check=True)
                pe.matmul(sc[1][:, 0:D], v_b_wide[0:R, 1, :], proj_w_f[0:R, 1, :], start=False, stop=True, skip_group_check=True)
                pe.matmul(sc[1][:, D:D + E], enc_b_wide, sw_w_f, start=False, stop=True,
                          skip_group_check=True).then_inc(folded, 1)

            def queries_keys(t):
                if isinstance(t, int) and t == 1:
                    pe.wait_ge(split_d, 2)
                pe.wait_ge(xnT_sb, t)
                at_least(pe, qk_lo, 2 * (t - 1))
                for j in range(3):
                    dst = qk01[:, j * PW:(j + 1) * PW] if j < 2 else qk2[:, 0:PW]
                    for n, (k, w) in enumerate(parts(qkv_h, qkv_l)):
                        mm = pe.matmul(dst, w[:, j * P:(j + 1) * P], xnT[:, k, :], start=(n == 0), stop=(n == 4))
                    if j > 0:
                        mm.then_inc(qk_ps, 1)

            def tokens(t):
                if isinstance(t, int) and t == 0:
                    pe.wait_ge(split_d, 1)
                    pe.wait_ge(zeroed_x, 1)
                pe.wait_ge(xT_sb, t + 1)
                at_least(pe, v_lo, t - 1)
                for g in range(2):
                    n = 0
                    for w in (tok_w_h, tok_w_l):
                        for half in range(2):
                            mm = pe.matmul(hv[:, g * D:(g + 1) * D], xT[:, g * P + half:g * P + half + P], w[:, half, :],
                                           start=(g == 0 and n == 0), stop=(n == 3), skip_group_check=True)
                            n += 1
                mm.then_inc(tok_ps, 1)

            def turn_x(t):
                if isinstance(t, int):
                    pe.wait_ge(x_lo, 1 if t < 1 else 2 if t < 4 else 4)
                at_least(pe, xnT_sb, t - 1)
                for g in range(2):
                    mm = pe.transpose(t0[:, 3, g * P:(g + 1) * P],
                                      x_s[:, ds(2 * t + g, 1)].rearrange("p o k c -> p (o k c)"), ident[:])
                mm.then_inc(xT_ps, 1)

            def scores_of(u, g):
                pe.matmul(sc[g][:, 0:H * TP], ident[:], causal[:].rearrange("p h s -> p (h s)"), start=True, stop=False,
                          skip_group_check=True)
                for rows, heads, j, k_of in ((slice(0, P), slice(0, HA * TP), 0, k_a), (slice(0, R), slice(HA * TP, H * TP), 2, k_b)):
                    for a, b in ((0, 0), (1, 0), (0, 1)):
                        for c in range(NB):
                            q = slice(g * P + c * TP, g * P + (c + 1) * TP)
                            mm = pe.matmul(sc[g][c * TP:(c + 1) * TP, heads], qk_s[u][rows, j, a, q], k_of[u][:, b, :, q],
                                           start=False, stop=(j == 2 and b == 1), skip_group_check=True)
                mm.then_inc(sc_ps, 1)

            def turn_x2(p):
                pe.wait_ge(x2_hi, p + 1)
                pe.wait_ge(x2_lo, p + 1)
                for g in range(2):
                    mm = turn(t1, x2_s[:, g].rearrange("p k d -> p (k d)"), g * P)
                mm.then_inc(x2T_ps, 1)

            def turn_y(p):
                pe.wait_ge(y_hi, p + 1)
                pe.wait_ge(y_lo, p + 1)
                at_least(pe, x2T_sb, p)
                for g in range(2):
                    mm = turn(t1, y_s[:, g].rearrange("p k d -> p (k d)"), g * P)
                mm.then_inc(yT_ps, 1)

            def project(p):
                if isinstance(p, int) and p == 0:
                    pe.wait_ge(split_d, 3)
                pe.wait_ge(yT_sb, p + 1)
                for g in range(2):
                    mm = rows_by_weights(yp[:, g * D:(g + 1) * D], yT, g * P, proj_h, proj_l, slice(0, D))
                mm.then_inc(proj_ps, 1)

            def logits(p, t):
                if isinstance(t, int) and t == 5:
                    pe.wait_ge(split_d, 4)
                pe.wait_ge(x2T_sb, p + 1)
                if isinstance(t, int) and t > NPAIR:
                    pe.wait_ge(logit_sb, p)
                    pe.wait_ge(v_lo, NPAIR)
                for g in range(2):
                    for n, (k, w) in enumerate(parts(router_h, router_l)):
                        mm = pe.matmul(hv[:, 2 * D + g * E:2 * D + (g + 1) * E], x2T[:, k, ds((2 * p + g) * P, P)], w,
                                       start=(n == 0), stop=(n == 4), skip_group_check=True)
                mm.then_inc(logit_ps, 1)

            def attend(p, v):
                pe.wait_ge(pT_bd, 16 * NB * (p + 1))
                at_least(pe, h2_sb, p)
                pe.wait_ge(v_lo, p + 1)
                for g in range(2):
                    for h_ in range(H):
                        o = (g * H + h_) * (HD + 1)
                        for n, (a, b) in enumerate(((0, 0), (1, 0), (0, 1))):
                            mm = pe.matmul(yp[:, o:o + HD + 1], p_bd[v][:, g, a, :, h_], v_s[v][:, g, b, h_, :],
                                           start=(g == 0 and h_ == 0 and n == 0), stop=(n == 2), skip_group_check=True)
                mm.then_inc(pv_ps, 1)

            def marks(s):
                for g in range(4):
                    mm = pe.transpose(t0[:, g // 2, (g % 2) * P:(g % 2 + 1) * P],
                                      onehot[:, ds(4 * s + g, 1), :].rearrange("p o c -> p (o c)"), ident[:])
                mm.then_inc(ohT_ps, 1)

            def first_product(s, u, j):
                dst = pre_bank(s, j)[:]
                at_least(pe, gh_sb, 4 * s + j - (1 if isinstance(s, int) and s < ALONE else 3))
                for n, (k, w) in enumerate(parts(w1_h, w1_l)[:4]):
                    pe.matmul(dst, w[:, j * P:(j + 1) * P], x2T[:, k, ds(s * BW, BW)], start=(n == 0), stop=False)
                if j == 0:
                    pe.wait_ge(ohT_sb, s + 1)
                    pe.wait_ge(x2c_sb, s + 1)
                pe.matmul(dst, w1_l[:, 1, j * P:(j + 1) * P], x2_oh[u][:], start=False, stop=True).then_inc(pre_ps, 1)

            def step(t, u, i):
                if isinstance(t, int) and t == 0:
                    pe.wait_ge(consts, 3)
                    turn_x(0)
                tokens_first = isinstance(t, int) and t < 4
                if has(t, 0) and tokens_first:
                    tokens(t)
                if has(t, 1):
                    queries_keys(t)
                if has(t, 0) and not tokens_first:
                    tokens(t)
                if has(t, -1):
                    turn_x(t + 1)
                if isinstance(t, int) and t == 0:
                    fold()
                if has(t, 5):
                    turn_x2(t - 5)
                if has(t, 2):
                    if isinstance(t, int) and t == 2:
                        pe.wait_ge(consts, 8)
                        pe.wait_ge(folded, 3)
                        pe.wait_ge(folded_d, 1)
                    pe.wait_ge(k_bd[u], 16 * (HA + HB) * i)
                    at_least(pe, sc_sb, t - 2)
                    scores_of(u, 0)
                if has(t, 4):
                    turn_y(t - 4)
                if has(t, 2):
                    scores_of(u, 1)
                if has(t, 4):
                    project(t - 4)
                if has(t, 1):
                    pe.wait_ge(h_sb, t + 1 if not isinstance(t, int) else min(t + 1, NPAIR))
                    for g in range(2):
                        mm = rows_by_weights(hv[:, g * D:(g + 1) * D], xnT, g * P, qkv_h, qkv_l, slice(2 * D, 3 * D))
                    mm.then_inc(v_ps, 1)
                if has(t, 5):
                    logits(t - 5, t)
                if has(t, 0):
                    pe.wait_ge(xn_hi, t + 1)
                    pe.wait_ge(xn_lo, t + 1)
                    pe.wait_ge(xT_sb, t + 2 if not isinstance(t, int) else min(t + 2, NPAIR))
                    for g in range(2):
                        mm = turn(t0, xn_s[:, g].rearrange("p k d -> p (k d)"), g * P)
                    mm.then_inc(xnT_ps, 1)
                if isinstance(t, int) and t == NPAIR:
                    pe.wait_ge(consts, 11)
                    pe.wait_ge(split_d, 7)
                    pe.wait_ge(router_d, 9)
                    pe.wait_ge(xnT_sb, NPAIR)
                    pe.wait_ge(qk_lo, 2 * NPAIR)
                    marks(0)
                    first_product(0, 0, 0)
                    first_product(0, 0, 1)
                if has(t, 3):
                    attend(t - 3, 1 - u)

            attention(pe, step, DRAIN)

            def second_product(q, u, k):
                if k == 0:
                    pe.wait_ge(gl_sb, 4 * q + 4)
                    at_least(pe, o_sb, q)
                for g in (2 * k, 2 * k + 1):
                    dst = ffn[k][:, (g % 2) * D:(g % 2 + 1) * D]
                    c = slice(g * P, (g + 1) * P)
                    pe.matmul(dst, x2_oh[u][:, c], b2_parts[:], start=(g % 2 == 0), stop=False, skip_group_check=True)
                    for j in range(4):
                        pe.matmul(dst, g_h[u][:, j, c], w2_h[:, j, :], start=False, stop=False, skip_group_check=True)
                        pe.matmul(dst, g_l[u][:, j, c], w2_h[:, j, :], start=False, stop=False, skip_group_check=True)
                        mm = pe.matmul(dst, g_h[u][:, j, c], w2_l[:, j, :], start=False, stop=(j == 3), skip_group_check=True)
                mm.then_inc(ffn_ps, 1)

            def ffn_step(s, u, i):
                if not isinstance(s, int) or s < NBLK:
                    marks(s)
                    for j in range(4):
                        first_product(s, u, j)
                for k in range(2):
                    second_product(s - 1, 1 - u, k)

            pe.wait_ge(k_bd[1], 16 * (HA + HB) * (NPAIR // 2))
            pe.wait_ge(sc_sb, NPAIR - 1)
            for g in range(2):
                scores_of(1, g)
            turn_x2(NPAIR - 4)
            turn_y(NPAIR - 3)
            project(NPAIR - 3)
            logits(NPAIR - 4, DRAIN)
            attend(NPAIR - 2, 0)
            pe.wait_ge(sc_sb, NPAIR)
            first_product(0, 0, 2)
            turn_x2(NPAIR - 3)
            first_product(0, 0, 3)
            turn_y(NPAIR - 2)
            second_product(0, 0, 0)
            project(NPAIR - 2)
            logits(NPAIR - 3, DRAIN + 1)
            marks(1)
            attend(NPAIR - 1, (NPAIR - 1) % 2)
            second_product(0, 0, 1)
            first_product(1, 1, 0)
            turn_x2(NPAIR - 2)
            first_product(1, 1, 1)
            turn_y(NPAIR - 1)
            first_product(1, 1, 2)
            project(NPAIR - 1)
            logits(NPAIR - 2, DRAIN + 2)
            first_product(1, 1, 3)
            marks(2)
            first_product(2, 0, 0)
            second_product(1, 1, 0)
            turn_x2(NPAIR - 1)
            first_product(2, 0, 1)
            second_product(1, 1, 1)
            logits(NPAIR - 1, DRAIN + 3)
            first_product(2, 0, 2)
            first_product(2, 0, 3)
            pe.wait_ge(logit_sb, NPAIR)
            pe.wait_ge(h2_sb, NPAIR)
            ffn_step(3, 1, 1)
            pe.wait_ge(router_d, 12 + 9)
            with pe.Fori(2, NBLK // 2) as i:
                for u in range(2):
                    ffn_step(2 * i + u, u, i)
            ffn_step(NBLK, 0, NBLK // 2)


def kernel(x, L0_tok_W, L0_tok_b, L0_attn_W_attn, L0_attn_b_attn, L0_attn_W_proj, L0_attn_b_proj,
           L0_ffn_enc_w, L0_ffn_enc_b, L0_ffn_sw_w, L0_ffn_sw_b, L0_ffn_w1, L0_ffn_b1, L0_ffn_w2, L0_ffn_b2):
    import numpy as np
    import concourse.bacc as bacc
    from concourse.bass_utils import run_bass_kernel_spmd

    def stack(w):
        a = [w[0:64], w[64:128], w[128:192]]
        return np.stack([np.concatenate([a[0], a[1]]), np.concatenate([a[2], a[0]]), np.concatenate([a[1], a[2]])], axis=1)

    inputs = [np.asarray(v) for v in (x, L0_tok_W, L0_tok_b, L0_attn_W_attn, L0_attn_b_attn, L0_attn_W_proj, L0_attn_b_proj,
                                      L0_ffn_enc_w, L0_ffn_enc_b, L0_ffn_sw_w, L0_ffn_sw_b, L0_ffn_w1, L0_ffn_b1, L0_ffn_w2, L0_ffn_b2)]
    x, tok_W, tok_b, W_attn, b_attn, W_proj, b_proj, enc_w, enc_b, sw_w, sw_b, w1, b1, w2, b2 = inputs
    order = np.concatenate([np.arange(0, 128), np.arange(192, 320), np.arange(128, 192), np.arange(320, 384), np.arange(384, 576)])
    halves = [tok_W[:, 0:CH].T, tok_W[:, CH:].T]
    vb = b_attn[384:]
    first = np.zeros((P, FIRST), np.float32)
    first[:, 0:D] = tok_b
    first[:, D:D + 3] = b_attn[order[:384]].reshape(3, P).T
    first[:, D + 3:D + 7] = b1.reshape(4, P).T
    later = np.zeros((P, LATER), np.float32)
    later[:, 0:D] = b_proj
    later[:, D:D + E] = sw_b
    later[:, 200:328] = vb[0:128, None]
    later[0:R, 328:456] = vb[128:192, None]
    later[0:R, 456:584] = enc_b[:, None]
    later[0:R, 584:592] = sw_w
    later[0:R, 592:976] = np.concatenate([stack(enc_w)[:, n].T for n in range(3)], axis=1)
    later[96:96 + E, 976:1168] = b2
    later[96 + E:96 + 2 * E, 976:1168] = b2
    arrays = {
        "x": x,
        "tok_w": np.stack([np.concatenate([w, w]) for w in halves], axis=1),
        "first_rows": first,
        "qkv_w": stack(W_attn[:, order]),
        "proj_w": stack(W_proj),
        "later_rows": later,
        "w1": stack(w1.transpose(1, 0, 2).reshape(D, ER)),
        "w2": w2.reshape(4, P, D).transpose(1, 0, 2),
    }
    nc = bacc.Bacc("TRN2", target_bir_lowering=False, num_devices=1)
    feeds, args = {}, []
    for name, a in arrays.items():
        feeds[name + "_dram"] = np.ascontiguousarray(a)
        args.append(nc.dram_tensor(name + "_dram", a.shape, F32, kind="ExternalInput").ap())
    out = nc.dram_tensor("out_dram", (B, T, D), F32, kind="ExternalOutput").ap()
    audio_tower(nc, *args, out)
    result = run_bass_kernel_spmd(nc, [feeds], core_ids=[0])
    return result.results[0]["out_dram"]
```
